# Optimizing a Trainium2 kernel written in Bass

```python
import numpy as np
import jax
import jax.numpy as jnp

def _softmax(x, axis=-1):
    return jax.nn.softmax(x, axis=axis)

def _gelu(x):
    return jax.nn.gelu(x, approximate=True)

def _silu(x):
    return jax.nn.silu(x)

def _sigmoid(x):
    return jax.nn.sigmoid(x)

def _layernorm(x, axis=-1, eps=1e-05):
    m = jnp.mean(x, axis=axis, keepdims=True)
    v = jnp.var(x, axis=axis, keepdims=True)
    return (x - m) / jnp.sqrt(v + eps)

def _scatter_add(tgt, idx, src, axis=0):
    return tgt.at[idx].add(src)

def _segment_sum(src, seg, n):
    return jax.ops.segment_sum(src, seg, n)
kernel_name = 'mk_gps_d1_gnn_r8_9b27e5'

def setup_inputs(seed: int=0):
    np.random.seed(seed)
    _w = jnp.asarray

    def _rec_inputs():
        import jax
        import jax.numpy as jnp
        _gk = jax.random.key(seed)
        x = -0.0003713 + 1 * jax.random.normal(jax.random.fold_in(_gk, 1), (12500, 256), jnp.float32)
        src = jax.random.randint(jax.random.fold_in(_gk, 2), (200000,), 0, 12500, jnp.int32)
        dst = jax.random.randint(jax.random.fold_in(_gk, 3), (200000,), 0, 12500, jnp.int32)
        _o = jnp.argsort(dst, stable=True)
        src = src[_o]
        dst = dst[_o]
        edge_type_8 = jax.random.randint(jax.random.fold_in(_gk, 12), (200000,), 0, 8, jnp.int32)
        edge_weight = jax.random.uniform(jax.random.fold_in(_gk, 13), (200000,), jnp.float32, 0.0, 0.999999)
        return (x, src, dst, edge_type_8, edge_weight)
    x, src, dst, edge_type_8, edge_weight = _rec_inputs()

    def _L0_gnn_setup():
        import jax, jax.numpy as jnp
        import numpy as np
        N_NODES = 6250
        N_EDGES = 75000
        C_IN = 256
        C_OUT = 256
        N_REL = 8
        key = jax.random.key(seed)
        ks = jax.random.split(key, 7)
        x = jax.random.normal(ks[0], (N_NODES, C_IN), dtype=jnp.float32)
        edge_index = jax.random.randint(ks[1], (2, N_EDGES), 0, N_NODES, dtype=jnp.int64)
        edge_type = jax.random.randint(ks[2], (N_EDGES,), 0, N_REL, dtype=jnp.int64)
        edge_weight = jax.random.uniform(ks[3], (N_EDGES,), dtype=jnp.float32)
        weight = jax.random.normal(ks[4], (N_REL, C_IN, C_OUT), dtype=jnp.float32) * (1.0 / np.sqrt(C_IN))
        root = jax.random.normal(ks[5], (C_IN, C_OUT), dtype=jnp.float32) * (1.0 / np.sqrt(C_IN))
        bias = jnp.zeros((C_OUT,), dtype=jnp.float32)
        return {'x': x, 'edge_index': edge_index, 'edge_type': edge_type, 'edge_weight': edge_weight, 'weight': weight, 'root': root, 'bias': bias}
    _L0_gnn_all = _L0_gnn_setup()
    _L0_gnn_in = {k: v for k, v in _L0_gnn_all.items() if k in ('weight', 'root', 'bias')}
    del _L0_gnn_all

    def _L0_mix_setup():
        import jax, jax.numpy as jnp
        import numpy as np
        D_MODEL = 256
        NUM_HEADS = 8
        DEPTH = D_MODEL // NUM_HEADS
        B, L = (32, 512)

        def _feature_map(x):
            return jax.nn.elu(x) + 1.0
        key = jax.random.key(seed)
        ks = jax.random.split(key, 9)
        sc = 1.0 / np.sqrt(D_MODEL)
        return {'x': jax.random.normal(ks[0], (B, L, D_MODEL), dtype=jnp.float32), 'wq': jax.random.normal(ks[1], (D_MODEL, D_MODEL), dtype=jnp.float32) * sc, 'bq': jnp.zeros((D_MODEL,), dtype=jnp.float32), 'wk': jax.random.normal(ks[2], (D_MODEL, D_MODEL), dtype=jnp.float32) * sc, 'bk': jnp.zeros((D_MODEL,), dtype=jnp.float32), 'wv': jax.random.normal(ks[3], (D_MODEL, D_MODEL), dtype=jnp.float32) * sc, 'bv': jnp.zeros((D_MODEL,), dtype=jnp.float32), 'wo': jax.random.normal(ks[4], (D_MODEL, D_MODEL), dtype=jnp.float32) * sc, 'bo': jnp.zeros((D_MODEL,), dtype=jnp.float32)}
    _L0_mix_all = _L0_mix_setup()
    _L0_mix_in = {k: v for k, v in _L0_mix_all.items() if k in ('wq', 'bq', 'wk', 'bk', 'wv', 'bv', 'wo', 'bo')}
    del _L0_mix_all

    def _L0_ffn_setup():
        import jax, jax.numpy as jnp
        import numpy as np
        E, D, H, TOP_K = (6, 256, 256, 2)
        ROUTER_H = D // 2
        key = jax.random.key(seed)
        ks = jax.random.split(key, 12)
        s = 1.0 / np.sqrt(D)
        sh = 1.0 / np.sqrt(H)
        sr = 1.0 / np.sqrt(ROUTER_H)
        return {'features': jax.random.normal(ks[0], (8, 512, D), dtype=jnp.float32), 'router_w1': jax.random.uniform(ks[1], (D, ROUTER_H), jnp.float32, -s, s), 'router_b1': jnp.zeros((ROUTER_H,), jnp.float32), 'router_w2': jax.random.uniform(ks[2], (ROUTER_H, E), jnp.float32, -sr, sr), 'router_b2': jnp.zeros((E,), jnp.float32), 'expert_w1': jax.random.uniform(ks[3], (E, D, H), jnp.float32, -s, s), 'expert_b1': jnp.zeros((E, H), jnp.float32), 'expert_w2': jax.random.uniform(ks[4], (E, H, H), jnp.float32, -sh, sh), 'expert_b2': jnp.zeros((E, H), jnp.float32), 'expert_w3': jax.random.uniform(ks[5], (E, H, D), jnp.float32, -sh, sh), 'expert_b3': jnp.zeros((E, D), jnp.float32)}
    _L0_ffn_all = _L0_ffn_setup()
    _L0_ffn_in = {k: v for k, v in _L0_ffn_all.items() if k in ('router_w1', 'router_b1', 'router_w2', 'router_b2', 'expert_w1', 'expert_b1', 'expert_w2', 'expert_b2', 'expert_w3', 'expert_b3')}
    del _L0_ffn_all
    return {'x': x, 'src': src, 'dst': dst, 'edge_type_8': edge_type_8, 'edge_weight': edge_weight, 'L0_gnn_weight': _L0_gnn_in['weight'], 'L0_gnn_root': _L0_gnn_in['root'], 'L0_gnn_bias': _L0_gnn_in['bias'], 'L0_mix_wq': _L0_mix_in['wq'], 'L0_mix_bq': _L0_mix_in['bq'], 'L0_mix_wk': _L0_mix_in['wk'], 'L0_mix_bk': _L0_mix_in['bk'], 'L0_mix_wv': _L0_mix_in['wv'], 'L0_mix_bv': _L0_mix_in['bv'], 'L0_mix_wo': _L0_mix_in['wo'], 'L0_mix_bo': _L0_mix_in['bo'], 'L0_ffn_router_w1': _L0_ffn_in['router_w1'], 'L0_ffn_router_b1': _L0_ffn_in['router_b1'], 'L0_ffn_router_w2': _L0_ffn_in['router_w2'], 'L0_ffn_router_b2': _L0_ffn_in['router_b2'], 'L0_ffn_expert_w1': _L0_ffn_in['expert_w1'], 'L0_ffn_expert_b1': _L0_ffn_in['expert_b1'], 'L0_ffn_expert_w2': _L0_ffn_in['expert_w2'], 'L0_ffn_expert_b2': _L0_ffn_in['expert_b2'], 'L0_ffn_expert_w3': _L0_ffn_in['expert_w3'], 'L0_ffn_expert_b3': _L0_ffn_in['expert_b3']}

def reference(x, src, dst, edge_type_8, edge_weight, L0_gnn_weight, L0_gnn_root, L0_gnn_bias, L0_mix_wq, L0_mix_bq, L0_mix_wk, L0_mix_bk, L0_mix_wv, L0_mix_bv, L0_mix_wo, L0_mix_bo, L0_ffn_router_w1, L0_ffn_router_b1, L0_ffn_router_w2, L0_ffn_router_b2, L0_ffn_expert_w1, L0_ffn_expert_b1, L0_ffn_expert_w2, L0_ffn_expert_b2, L0_ffn_expert_w3, L0_ffn_expert_b3):
    import jax
    import jax.numpy as jnp

    def _L0_gnn_ref(x, edge_index, edge_type, edge_weight, weight, root, bias):
        import jax, jax.numpy as jnp
        import numpy as np
        N_NODES = 6250
        N_EDGES = 75000
        C_IN = 256
        C_OUT = 256
        N_REL = 8
        "RGCNConv (no bases/blocks), aggr='mean', root_weight=True, bias=True.\n\n            Equivalent to the PyG per-relation loop:\n                for r: out += scatter_mean(x[src_r] * w_r, dst_r) @ weight[r]\n                out += x @ root + bias\n            but fused: one segmented mean over (relation, dst) pairs followed by a\n            grouped GEMM over relations.\n            "
        N, C = x.shape
        R = weight.shape[0]
        src, dst = (edge_index[0], edge_index[1])
        msg = x[src] * edge_weight[:, None]
        seg = edge_type * N + dst
        sums = jax.ops.segment_sum(msg, seg, num_segments=R * N)
        cnt = jax.ops.segment_sum(jnp.ones_like(edge_weight), seg, num_segments=R * N)
        h = sums / jnp.maximum(cnt, 1.0)[:, None]
        h = h.reshape(R, N, C)
        out = jnp.einsum('rnc,rco->no', h, weight)
        out = out + x @ root + bias
        return out

    def _L0_mix_ref(x, wq, bq, wk, bk, wv, bv, wo, bo):
        import jax, jax.numpy as jnp
        import numpy as np
        D_MODEL = 256
        NUM_HEADS = 8
        DEPTH = D_MODEL // NUM_HEADS
        B, L = (32, 512)

        def _feature_map(x):
            return jax.nn.elu(x) + 1.0
        b, l, _ = x.shape
        q = (x @ wq + bq).reshape(b, l, NUM_HEADS, DEPTH)
        k = (x @ wk + bk).reshape(b, l, NUM_HEADS, DEPTH)
        v = (x @ wv + bv).reshape(b, l, NUM_HEADS, DEPTH)
        q = _feature_map(q)
        k = _feature_map(k)
        kv = jnp.einsum('blhd,blhe->bhde', k, v)
        k_sum = jnp.sum(k, axis=1)
        qkv = jnp.einsum('blhd,bhde->blhe', q, kv)
        normalizer = jnp.einsum('blhd,bhd->blh', q, k_sum) + 1e-06
        out = qkv / normalizer[..., None]
        out = out.reshape(b, l, D_MODEL)
        return out @ wo + bo

    def _L0_ffn_ref(features, router_w1, router_b1, router_w2, router_b2, expert_w1, expert_b1, expert_w2, expert_b2, expert_w3, expert_b3):
        import jax, jax.numpy as jnp
        import numpy as np
        E, D, H, TOP_K = (6, 256, 256, 2)
        ROUTER_H = D // 2
        rh = jax.nn.relu(features @ router_w1 + router_b1)
        expert_logits = jax.nn.softmax(rh @ router_w2 + router_b2, axis=-1)
        top_w, top_i = jax.lax.top_k(expert_logits, TOP_K)
        routing_weights = jax.nn.softmax(top_w, axis=-1)
        h1 = jax.nn.relu(jnp.einsum('bsd,edh->bseh', features, expert_w1) + expert_b1)
        h2 = jax.nn.relu(jnp.einsum('bseh,ehf->bsef', h1, expert_w2) + expert_b2)
        expert_out = jnp.einsum('bsef,efo->bseo', h2, expert_w3) + expert_b3
        sel = jnp.take_along_axis(expert_out, top_i[:, :, :, None], axis=2)
        combined = jnp.sum(sel * routing_weights[..., None], axis=2)
        return combined
    edge_index = jnp.stack([src, dst])
    xn = _layernorm(x, axis=-1)
    x = x + _L0_gnn_ref(xn, edge_index, edge_type_8, edge_weight, L0_gnn_weight, L0_gnn_root, L0_gnn_bias) + _L0_mix_ref(xn[None], L0_mix_wq, L0_mix_bq, L0_mix_wk, L0_mix_bk, L0_mix_wv, L0_mix_bv, L0_mix_wo, L0_mix_bo)[0]
    x = x + _L0_ffn_ref(_layernorm(x, axis=-1)[None], L0_ffn_router_w1, L0_ffn_router_b1, L0_ffn_router_w2, L0_ffn_router_b2, L0_ffn_expert_w1, L0_ffn_expert_b1, L0_ffn_expert_w2, L0_ffn_expert_b2, L0_ffn_expert_w3, L0_ffn_expert_b3)[0]
    return x

_drawn_inputs = setup_inputs


def setup_inputs(seed=0):
    import zlib

    import numpy as np

    out = dict(_drawn_inputs(seed))
    spreads = {'L0_gnn_bias': (0.0, 0.1),
     'L0_mix_bq': (0.0, 0.8),
     'L0_mix_bk': (0.0, 0.8),
     'L0_mix_bv': (0.0, 0.1),
     'L0_mix_bo': (0.0, 0.1),
     'L0_ffn_router_b1': (0.0, 0.384),
     'L0_ffn_router_b2': (0.0, 0.1),
     'L0_ffn_expert_b1': (0.0, 0.8),
     'L0_ffn_expert_b2': (0.0, 0.524),
     'L0_ffn_expert_b3': (0.0, 0.1)}
    factors = {'L0_mix_wq': 8.0, 'L0_mix_wk': 8.0, 'L0_mix_wv': 6.899}
    for name, (base, spread) in spreads.items():
        noise = np.random.default_rng([zlib.crc32(name.encode()), seed]).standard_normal(out[name].shape)
        drawn = base * np.exp(spread * noise) if base else spread * noise
        out[name] = jnp.asarray(drawn.astype(out[name].dtype))
    for name, factor in factors.items():
        out[name] = (out[name] * factor).astype(out[name].dtype)
    return out
```

```python
import concourse.bass as bass
from concourse import mybir
from concourse.alu_op_type import AluOpType as ALU
from contextlib import ExitStack

F32 = mybir.dt.float32
BF16 = mybir.dt.bfloat16
I32 = mybir.dt.int32
ACT = mybir.ActivationFunctionType
AX = mybir.AxisListType

N, C, E, REL = 12500, 256, 200000, 8
HEADS, EXPERTS = 8, 6
P = 128
KC = C // P
SUPER = 25
NS = N // SUPER
SUB = 4
NT = NS // SUB
STEPS = SUPER * SUB
BT = 4
BE = BT * P
REAL_BLOCKS = -(-E // BE)
UNIT = 4
BLOCKS = STEPS * UNIT
TILES = BLOCKS * BT
UT = UNIT * BT
WIN = 64
MAXW = -(-NS // WIN)
SLOTS = 9
CHUNK = 3
LN_EPS = 1e-5
DEN_EPS = 1e-6


def gps_layer(nc, x, src, dst, etype, ew, g_w, g_root, g_b, wq, bq, wk, bk, wv, bv, wo, bo,
              r_w1, r_b1, r_w2, r_b2, e_w1, e_b1, e_w2, e_b2, e_w3, e_b3, out):
    assert BLOCKS >= REAL_BLOCKS and N == SUPER * SUB * NT
    y_tab = nc.dram_tensor("y_tab", [REL * N, C], F32).ap()
    xt_tab = nc.dram_tensor("xt_tab", [SUPER, P, SUB * KC * NT], F32).ap()
    ty_tab = nc.dram_tensor("ty_tab", [BLOCKS * BE], I32).ap()

    def load_row(eng, row, least, most):
        _, values = nc.values_load_multi_w_load_instructions(row, engines=(eng.engine,), min_val=least, max_val=most)
        return values

    whole = ExitStack()
    with whole:
        def sbuf(scope, name, shape, dt=F32):
            return scope.enter_context(nc.sbuf_tensor(name, shape, dt))

        def psum(scope, name, shape=(P, 512)):
            return scope.enter_context(nc.psum_tensor(name, list(shape), F32))

        def sem(name):
            return whole.enter_context(nc.semaphore(name))

        w1_sb = sbuf(whole, "w1_sb", [P, EXPERTS, KC, C])
        w2_sb = sbuf(whole, "w2_sb", [P, EXPERTS, KC, C])
        w3_sb = sbuf(whole, "w3_sb", [P, EXPERTS, KC, C])
        wq_sb = sbuf(whole, "wq_sb", [P, KC, C])
        wo_sb = sbuf(whole, "wo_sb", [P, KC, C])
        root_sb = sbuf(whole, "root_sb", [P, KC, C])
        rw1_sb = sbuf(whole, "rw1_sb", [P, KC, P])
        rw2_sb = sbuf(whole, "rw2_sb", [P, EXPERTS])
        rb2_sb = sbuf(whole, "rb2_sb", [P, EXPERTS])
        b3_sb = sbuf(whole, "b3_sb", [EXPERTS, C])
        ident = sbuf(whole, "ident", [P, P])
        head_mask = sbuf(whole, "head_mask", [P, P])
        iota_w = sbuf(whole, "iota_w", [P, WIN])
        ones = sbuf(whole, "ones", [P, P])
        eps_ln = sbuf(whole, "eps_ln", [P, 1])
        eps_den = sbuf(whole, "eps_den", [P, 1])
        BQ, GB, BO, RB1, EB1, EB2, NB = 0, 2, 4, 6, 7, 19, 31
        bias_rows = sbuf(whole, "bias_rows", [32, P])
        bias_t = sbuf(whole, "bias_t", [P, 32])
        out_bias = sbuf(whole, "out_bias", [P, KC])
        dst_t = sbuf(whole, "dst_t", [P, TILES])
        coef_t = sbuf(whole, "coef_t", [P, TILES])
        idx_t = sbuf(whole, "idx_t", [P, TILES], I32)
        vmin_b = sbuf(whole, "vmin_b", [P, BLOCKS])
        lo_row = sbuf(whole, "lo_row", [1, SUPER], I32)
        hi_row = sbuf(whole, "hi_row", [1, SUPER], I32)
        nwin_row = sbuf(whole, "nwin_row", [1, BLOCKS], I32)
        nwu_row = sbuf(whole, "nwu_row", [1, STEPS], I32)
        kv_bd = sbuf(whole, "kv_bd", [P, KC, P])
        ksum_bd = sbuf(whole, "ksum_bd", [P, KC, P])

        pro = ExitStack()
        early = ExitStack()
        type_t = sbuf(early, "type_t", [P, TILES])
        rel0_t = sbuf(early, "rel0_t", [P, TILES])
        base0_row = sbuf(early, "base0_row", [1, BLOCKS], I32)
        wt_t = sbuf(early, "wt_t", [P, TILES])
        wrel_sb = sbuf(early, "wrel_sb", [P, KC, REL, C])
        iota_r = sbuf(early, "iota_r", [P, REL])
        iota_p = sbuf(early, "iota_p", [REL, 1])
        with pro:
            BC = 4
            LAST = BLOCKS - 3 * P
            FULL = E // BE - 3 * P
            REST = E - (E // BE) * BE
            raw_i = sbuf(pro, "raw_i", [P, 3, BC, BE], I32)
            f_rows = sbuf(pro, "f_rows", [P, 3, BC, BE])
            w_rows = sbuf(pro, "w_rows", [P, BC, BE])
            neg_i = sbuf(pro, "neg_i", [P, P], I32)
            vmm = sbuf(pro, "vmm", [P, 2, BC])
            diag = sbuf(pro, "diag", [P, 2, BC, P])
            vmax_b = sbuf(pro, "vmax_b", [P, BLOCKS])
            sstart = sbuf(pro, "sstart", [P, 1])
            send = sbuf(pro, "send", [P, 1])
            bid = sbuf(pro, "bid", [P, BLOCKS])
            below = sbuf(pro, "below", [P, BLOCKS])
            over = sbuf(pro, "over", [P, BLOCKS])
            cand = sbuf(pro, "cand", [P, 2, BLOCKS])
            lohi = sbuf(pro, "lohi", [P, 2])
            some = sbuf(pro, "some", [P, 1])
            span = sbuf(pro, "span", [1, BLOCKS])
            span_i = sbuf(pro, "span_i", [1, BLOCKS], I32)
            nw_f = sbuf(pro, "nw_f", [1, BLOCKS])
            nwu_f = sbuf(pro, "nwu_f", [1, STEPS])
            tp = [psum(pro, f"tp{i}") for i in range(2)]
            pmin, pmax, prow, pbias = (psum(pro, n) for n in ("pmin", "pmax", "prow", "pbias"))

            edges_in, pads_set, weights_in, small_in, ty_in = (
                sem(n) for n in ("edges_in", "pads_set", "weights_in", "small_in", "ty_in"))
            ident_set, consts_set, rows_done, vmm_done = (
                sem(n) for n in ("ident_set", "consts_set", "rows_done", "vmm_done"))
            tp_full, tp_free, spread_done, row_ready, row_done, bias_full = (
                sem(n) for n in ("tp_full", "tp_free", "spread_done", "row_ready", "row_done", "bias_full"))

            flat_n = 3 * P * BE

            def by_block(a):
                return a[0:flat_n].rearrange("(c p k) -> p c k", p=P, k=BE)

            block = pro.enter_context(nc.Block())

            @block.sync
            def _(sp):
                sp.wait_ge(pads_set, 1)
                n = 0
                for i, a in enumerate((dst, etype, src)):
                    sp.dma_start(raw_i[:, i, 0:3, :], by_block(a)).then_inc(edges_in, 16)
                    sp.dma_start(raw_i[0:FULL, i, 3, :],
                                 a[flat_n:flat_n + FULL * BE].rearrange("(p k) -> p k", k=BE)).then_inc(edges_in, 16)
                    sp.dma_start(raw_i[FULL:FULL + 1, i, 3, 0:REST],
                                 a[E - REST:E].rearrange("(p k) -> p k", p=1)).then_inc(edges_in, 16)
                    n += 3
                sp.dma_start(raw_i[FULL:FULL + 1, 0, 3, REST:BE],
                             dst[E - (BE - REST):E].rearrange("(p k) -> p k", p=1)).then_inc(edges_in, 16)
                sp.dma_start(w_rows[:, 0:3, :], by_block(ew)).then_inc(edges_in, 16)
                sp.dma_start(w_rows[0:FULL, 3, :],
                             ew[flat_n:flat_n + FULL * BE].rearrange("(p k) -> p k", k=BE)).then_inc(edges_in, 16)
                sp.dma_start(w_rows[FULL:FULL + 1, 3, 0:REST],
                             ew[E - REST:E].rearrange("(p k) -> p k", p=1)).then_inc(edges_in, 16)
                pad = BLOCKS * BE - E
                rows = 48
                sp.dma_start(ty_tab[0:E].rearrange("(a k) -> a k", a=16),
                             etype.rearrange("(a k) -> a k", a=16)).then_inc(ty_in, 16)
                sp.dma_start(ty_tab[E:BLOCKS * BE].rearrange("(a k) -> a k", a=rows),
                             neg_i[0:rows, 0:pad // rows]).then_inc(ty_in, 16)
                sp.wait_ge(ty_in, 32)

            EDGES_IN = 16 * 13

            @block.scalar
            def _(act):
                def two(w):
                    return w.rearrange("(k p) n -> p k n", p=P)
                act.dma_start(bias_rows[BQ:BQ + 2, :], bq.rearrange("(k p) -> k p", p=P)).then_inc(small_in, 16)
                act.dma_start(bias_rows[GB:GB + 2, :], g_b.rearrange("(k p) -> k p", p=P)).then_inc(small_in, 16)
                act.dma_start(bias_rows[BO:BO + 2, :], bo.rearrange("(k p) -> k p", p=P)).then_inc(small_in, 16)
                act.dma_start(bias_rows[RB1:RB1 + 1, :], r_b1.rearrange("(k p) -> k p", p=P)).then_inc(small_in, 16)
                act.dma_start(bias_rows[EB1:EB1 + 12, :], e_b1.rearrange("e (k p) -> (e k) p", p=P)).then_inc(small_in, 16)
                act.dma_start(bias_rows[EB2:EB2 + 12, :], e_b2.rearrange("e (k p) -> (e k) p", p=P)).then_inc(small_in, 16)
                act.dma_start(rb2_sb[:, :], r_b2.rearrange("(a n) -> a n", a=1).to_broadcast([P, EXPERTS])).then_inc(weights_in, 16)
                act.dma_start(wq_sb[:, :, :], two(wq)).then_inc(weights_in, 16)
                act.dma_start(wo_sb[:, :, :], two(wo)).then_inc(weights_in, 16)
                act.dma_start(root_sb[:, :, :], two(g_root)).then_inc(weights_in, 16)
                act.dma_start(rw1_sb[:, :, :], two(r_w1)).then_inc(weights_in, 16)
                act.dma_start(rw2_sb[:, :], r_w2).then_inc(weights_in, 16)
                act.dma_start(b3_sb[:, :], e_b3).then_inc(weights_in, 16)
                for k in range(KC):
                    act.dma_start(wrel_sb[:, k, :, :],
                                  g_w[:, k * P:(k + 1) * P, :].rearrange("r p n -> p r n")).then_inc(weights_in, 16)
                for w_d, w_s in ((e_w1, w1_sb), (e_w2, w2_sb), (e_w3, w3_sb)):
                    for k in range(KC):
                        act.dma_start(w_s[:, :, k, :],
                                      w_d[:, k * P:(k + 1) * P, :].rearrange("e p n -> p e n")).then_inc(weights_in, 16)
                act.wait_ge(weights_in, 16 * (7 + 2 + 6))

            @block.gpsimd
            def _(pool):
                pool.memset(raw_i[:, :, 3, :], -1)
                pool.memset(neg_i[:, :], -1)
                pool.memset(w_rows[:, 3, :], 0.0).then_inc(pads_set, 1)
                pool.memset(ident[:, :], 0.0).then_inc(ident_set, 1)
                pool.wait_ge(ident_set, 1)
                pool.affine_select(out=ident[:, :], in_=ident[:, :], compare_op=ALU.not_equal, fill=1.0,
                                   base=0, pattern=[[-1, P]], channel_multiplier=1).then_inc(ident_set, 1)
                pool.memset(ones[:, :], 1.0)
                pool.memset(eps_ln[:, :], LN_EPS)
                pool.memset(eps_den[:, :], DEN_EPS)
                pool.memset(head_mask[:, :], 0.0)
                pool.iota(iota_w[:, :], pattern=[[1, WIN]], base=0, channel_multiplier=0,
                          allow_small_or_imprecise_dtypes=True)
                pool.iota(iota_r[:, :], pattern=[[1, REL]], base=0, channel_multiplier=0,
                          allow_small_or_imprecise_dtypes=True)
                pool.iota(iota_p[:, :], pattern=[[0, 1]], base=0, channel_multiplier=1,
                          allow_small_or_imprecise_dtypes=True)
                pool.iota(sstart[:, :], pattern=[[0, 1]], base=0, channel_multiplier=NS,
                          allow_small_or_imprecise_dtypes=True)
                pool.iota(send[:, :], pattern=[[0, 1]], base=NS, channel_multiplier=NS,
                          allow_small_or_imprecise_dtypes=True)
                pool.iota(bid[:, :], pattern=[[1, BLOCKS]], base=0, channel_multiplier=0,
                          allow_small_or_imprecise_dtypes=True).then_inc(consts_set, 1)

            @block.vector
            def _(dve):
                dve.wait_ge(edges_in, EDGES_IN)
                dve.wait_ge(consts_set, 1)
                dve.wait_ge(ident_set, 2)
                dve.tensor_copy(f_rows[:, 0, :, :], raw_i[:, 0, :, :])
                dve.tensor_copy(f_rows[:, 1, :, :], raw_i[:, 1, :, :])
                dve.drain()
                dve.scalar_tensor_tensor(out=f_rows[:, 2, :, :], in0=f_rows[:, 1, :, :], scalar=float(N),
                                         in1=raw_i[:, 2, :, :], op0=ALU.mult, op1=ALU.add)
                for h in range(4):
                    dve.memset(head_mask[32 * h:32 * h + 32, 32 * h:32 * h + 32], 1.0)
                dve.drain()
                dve.tensor_scalar(f_rows[:, 2, :, :], f_rows[:, 2, :, :], 0.0, None, ALU.max).then_inc(rows_done, 1)
                dve.tensor_reduce(vmm[:, 0, :], f_rows[:, 0, :, :], AX.X, ALU.min)
                dve.tensor_reduce(vmm[:, 1, :], f_rows[:, 0, :, :], AX.X, ALU.max)
                dve.drain()
                for i in range(2):
                    for c in range(BC):
                        last = dve.tensor_scalar(diag[:, i, c, :], ident[:, :], vmm[:, i, c:c + 1], None, ALU.mult)
                last.then_inc(vmm_done, 1)
                n = 0
                for c in range(BC):
                    nb = P if c < 3 else LAST
                    for a, dest in enumerate((dst_t, type_t, idx_t, wt_t)):
                        dve.wait_ge(tp_full, n + 1)
                        o = dest[:, c * BE:c * BE + nb * BT].rearrange("p (b q) -> p q b", q=BT)
                        i = tp[n % 2][:, :].rearrange("p (q b) -> p q b", q=BT)[:, :, 0:nb]
                        dve.tensor_copy(o, i).then_inc(tp_free, 1)
                        n += 1
                dve.wait_ge(spread_done, 1)
                dve.tensor_scalar(vmin_b[:, :], pmin[:, 0:BLOCKS], 0.0, None, ALU.max)
                dve.tensor_copy(vmax_b[:, :], pmax[:, 0:BLOCKS])
                dve.drain()
                dve.tensor_tensor(rel0_t[:, :].rearrange("p (b t) -> p b t", t=BT),
                                  dst_t[:, :].rearrange("p (b t) -> p b t", t=BT),
                                  vmin_b[:, :].unsqueeze(2).to_broadcast([P, BLOCKS, BT]), ALU.subtract)
                dve.tensor_copy(base0_row[:, :], vmin_b[0:1, :])
                dve.tensor_scalar(below[:, :], vmin_b[:, :], send[:, 0:1], None, ALU.is_lt)
                dve.drain()
                dve.scalar_tensor_tensor(out=over[:, :], in0=vmax_b[:, :], scalar=sstart[:, 0:1],
                                         in1=below[:, :], op0=ALU.is_ge, op1=ALU.mult)
                dve.drain()
                dve.scalar_tensor_tensor(out=cand[:, 0, :], in0=over[:, :], scalar=-1000.0, in1=bid[:, :],
                                         op0=ALU.mult, op1=ALU.add)
                dve.scalar_tensor_tensor(out=cand[:, 1, :], in0=bid[:, :], scalar=1.0, in1=over[:, :],
                                         op0=ALU.add, op1=ALU.mult)
                dve.drain()
                dve.tensor_reduce(lohi[:, 0:1], cand[:, 0, :], AX.X, ALU.min)
                dve.tensor_reduce(lohi[:, 1:2], cand[:, 1, :], AX.X, ALU.max)
                dve.drain()
                dve.tensor_scalar(some[:, :], lohi[:, 1:2], 1.0, None, ALU.min)
                dve.tensor_scalar(lohi[:, 0:1], lohi[:, 0:1], 1000.0, None, ALU.add)
                dve.drain()
                dve.tensor_tensor(lohi[:, 0:1], lohi[:, 0:1], some[:, :], ALU.mult)
                dve.tensor_scalar(lohi[:, 1:2], lohi[:, 1:2], 1.0, None, ALU.max).then_inc(row_ready, 1)
                dve.tensor_tensor(span[:, :], vmax_b[0:1, :], vmin_b[0:1, :], ALU.subtract)
                dve.drain()
                dve.tensor_scalar(span_i[:, :], span[:, :], 0.0, None, ALU.max)
                dve.drain()
                dve.tensor_single_scalar(span_i[:, :], span_i[:, :], WIN.bit_length() - 1, op=ALU.arith_shift_right)
                dve.drain()
                dve.tensor_scalar(nw_f[:, :], span_i[:, :], 1.0, None, ALU.add)
                dve.drain()
                dve.tensor_scalar(nwin_row[:, :], nw_f[:, :], float(MAXW), None, ALU.min)
                dve.tensor_reduce(nwu_f[:, :], nw_f[:, :].rearrange("p (u b) -> p u b", b=UNIT), AX.X, ALU.max)
                dve.drain()
                dve.tensor_copy(nwu_row[:, :], nwu_f[:, :])
                dve.wait_ge(row_done, 1)
                dve.tensor_copy(lo_row[:, :], prow[0:1, 0:SUPER])
                dve.tensor_copy(hi_row[:, :], prow[0:1, 32:32 + SUPER])
                dve.wait_ge(bias_full, 1)
                dve.tensor_copy(bias_t[:, 0:NB], pbias[:, 0:NB])
                dve.drain()
                dve.tensor_tensor(out_bias[:, :], bias_t[:, GB:GB + 2], bias_t[:, BO:BO + 2], ALU.add)

            @block.tensor
            def _(pe):
                pe.wait_ge(ident_set, 2)
                pe.wait_ge(consts_set, 1)
                pe.wait_ge(small_in, 16 * 6)
                pe.transpose(pbias[:, 0:NB], bias_rows[0:NB, :], ident[0:NB, 0:NB]).then_inc(bias_full, 1)
                pe.wait_ge(rows_done, 1)
                n = 0
                for c in range(BC):
                    nb = P if c < 3 else LAST
                    for a in range(4):
                        if n >= 2:
                            pe.wait_ge(tp_free, n - 1)
                        for q in range(BT):
                            s_ = (f_rows[0:nb, a, c, q * P:(q + 1) * P] if a < 3
                                  else w_rows[0:nb, c, q * P:(q + 1) * P])
                            last = pe.transpose(tp[n % 2][:, q * P:q * P + nb], s_, ident[0:nb, 0:nb])
                        last.then_inc(tp_full, 1)
                        n += 1
                pe.wait_ge(vmm_done, 1)
                for i, bank in enumerate((pmin, pmax)):
                    for c in range(BC):
                        nb = P if c < 3 else LAST
                        last = pe.matmul(bank[:, c * P:c * P + nb], ones[0:nb, :], diag[0:nb, i, c, 0:nb],
                                         start=True, stop=True)
                last.then_inc(spread_done, 1)
                pe.wait_ge(row_ready, 1)
                for i in range(2):
                    last = pe.matmul(prow[0:1, 32 * i:32 * i + SUPER], lohi[0:SUPER, i:i + 1],
                                     ident[0:SUPER, 0:SUPER], start=True, stop=True)
                last.then_inc(row_done, 1)

        cnt = sbuf(early, "cnt", [REL, N + WIN])
        pa = ExitStack()
        with pa:
            wkv_sb = sbuf(pa, "wkv_sb", [P, KC, 2 * C])
            bkv_sb = sbuf(pa, "bkv_sb", [P, 2 * C])
            xs = sbuf(pa, "xs", [P, SUB, C])
            stats = sbuf(pa, "stats", [P, SUB, 6])
            mv = sbuf(pa, "mv", [P, SUB, 2])
            std = sbuf(pa, "std", [P, SUB])
            rstd = sbuf(pa, "rstd", [P, SUB])
            nmr = sbuf(pa, "nmr", [P, SUB])
            xn = sbuf(pa, "xn", [P, SUB, C])
            xnt = sbuf(pa, "xnt", [P, SUB, KC, NT])
            zk = sbuf(pa, "zk", [P, 2, C])
            vx = sbuf(pa, "vx", [P, 2, KC, P + 1])
            ek = sbuf(pa, "ek", [P, 2, C])
            rk = sbuf(pa, "rk", [P, 2, C])
            kf = sbuf(pa, "kf", [P, 2, C])
            wofs = sbuf(pa, "wofs", [P, 1])
            basew = sbuf(pa, "basew", [P, UNIT])
            base_i = sbuf(pa, "base_i", [1, UNIT], I32)
            rel = sbuf(pa, "rel", [P, UT])
            sel = sbuf(pa, "sel", [P, UT, WIN], BF16)
            rsel = sbuf(pa, "rsel", [P, UT, REL], BF16)
            zero = sbuf(pa, "zero", [P, 2 * (P + 1)])
            tb = [psum(pa, f"tb{k}") for k in range(KC)]
            pproj = [psum(pa, f"pproj{i}") for i in range(2)]
            pkv, pcnt = (psum(pa, n) for n in ("pkv", "pcnt"))

            x_in, var_ready, std_ready, nmr_ready, xn_ready, tr_done, xnt_ready, xnt_stored = (
                sem(n) for n in ("x_in", "var_ready", "std_ready", "nmr_ready", "xn_ready", "tr_done", "xnt_ready",
                                 "xnt_stored"))
            proj_done, z_done, e_done, kf_done, kv_acc = (
                sem(n) for n in ("proj_done", "z_done", "e_done", "kf_done", "kv_acc"))
            sel_ready, cnt_mm, kv_zero, wkv_in, bkv_in = (
                sem(n) for n in ("sel_ready", "cnt_mm", "kv_zero", "wkv_in", "bkv_in"))

            block = pa.enter_context(nc.Block())

            @block.sync
            def _(sp):
                def load(s):
                    sp.dma_start(xs[0:NT, :, :], x[bass.ds(s * NS, NS), :].rearrange("(t p) c -> p t c", p=NT)
                                 ).then_inc(x_in, 16)

                def store(s):
                    sp.wait_ge(xnt_ready, s + 1)
                    sp.dma_start(xt_tab[bass.ds(s, 1), :, :].rearrange("a p n -> (a p) n"),
                                 xnt[:, :, :, :].rearrange("p t k n -> p (t k n)")).then_inc(xnt_stored, 16)

                sp.sem_inc(xnt_stored, 16)
                load(0)
                for i, (w, b) in enumerate(((wk, bk), (wv, bv))):
                    sp.dma_start(wkv_sb[:, :, i * C:(i + 1) * C], w.rearrange("(k p) n -> p k n", p=P)
                                 ).then_inc(wkv_in, 16)
                    sp.dma_start(bkv_sb[:, i * C:(i + 1) * C],
                                 b.rearrange("(a n) -> a n", a=1).to_broadcast([P, C])).then_inc(bkv_in, 16)
                with sp.Fori(0, SUPER - 1) as s:
                    sp.wait_ge(xn_ready, s + 1)
                    load(s + 1)
                    store(s)
                store(SUPER - 1)
                sp.wait_ge(xnt_stored, 16 * (SUPER + 1))

            @block.scalar
            def _(act):
                act.sem_inc(e_done, 2)

                def normalise(s):
                    act.wait_ge(var_ready, s + 1)
                    act.activation(std[0:NT, :], mv[0:NT, :, 1], ACT.Sqrt, bias=eps_ln[0:NT, :]).then_inc(std_ready, 1)
                    act.wait_ge(nmr_ready, s + 1)
                    for t in range(SUB):
                        last = act.activation(xn[0:NT, t, :], xs[0:NT, t, :], ACT.Identity,
                                              bias=nmr[0:NT, t:t + 1], scale=rstd[0:NT, t:t + 1])
                    last.then_inc(xn_ready, 1)

                def supertile(s, more):
                    act.wait_ge(tr_done, s + 1)
                    act.wait_ge(xnt_stored, 16 * (s + 1))
                    for k in range(KC):
                        last = act.activation(xnt[:, :, k, :], tb[k][:, 0:NS].rearrange("p (t n) -> p t n", t=SUB),
                                              ACT.Copy)
                    last.then_inc(xnt_ready, 1)
                    for t in range(SUB):
                        u = SUB * s + t
                        act.wait_ge(kf_done, u + 1)
                        act.wait_ge(z_done, u + 3)
                        act.activation(ek[0:NT, t % 2, :], zk[0:NT, t % 2, :], ACT.Exp)
                        act.activation(rk[0:NT, t % 2, :], zk[0:NT, t % 2, :], ACT.Relu).then_inc(e_done, 1)
                        if more and t == 1:
                            normalise(s + 1)

                normalise(0)
                with act.Fori(0, SUPER - 1) as s:
                    supertile(s, True)
                supertile(SUPER - 1, False)

            @block.gpsimd
            def _(pool):
                pool.sem_inc(kf_done, 2)
                steps = pool.alloc_register("kf_steps")
                pool.reg_mov(steps, 1)
                with pool.Fori(0, SUPER) as s:
                    for t in range(SUB):
                        h = t % 2
                        n = pool.snap(steps, min_val=1, max_val=STEPS)
                        pool.wait_ge(kv_acc, n)
                        pool.wait_ge(e_done, n + 2)
                        pool.reg_add(steps, steps, 1)
                        pool.tensor_scalar(ek[0:NT, h, :], ek[0:NT, h, :], 1.0, 0.0, ALU.min, ALU.max)
                        pool.drain()
                        pool.tensor_tensor(kf[0:NT, h, :], ek[0:NT, h, :], rk[0:NT, h, :], ALU.add).then_inc(kf_done, 1)

            @block.vector
            def _(dve):
                dve.memset(cnt[:, :], 0.0)
                dve.memset(vx[:, :, :, :], 1.0)
                dve.memset(zero[:, :], 0.0).then_inc(kv_zero, 1)
                dve.sem_inc(z_done, 2)
                qa = dve.alloc_register("count_passes")
                dve.reg_mov(qa, 1)

                def statistics(s):
                    dve.wait_ge(x_in, 16 * (s + 1))
                    for t in range(SUB):
                        dve.bn_stats(stats[0:NT, t, :], xs[0:NT, t, :])
                    dve.drain()
                    for t in range(SUB):
                        last = dve.bn_aggr(mv[0:NT, t, :], stats[0:NT, t, :])
                    last.then_inc(var_ready, 1)

                def scales(s):
                    dve.wait_ge(std_ready, s + 1)
                    dve.reciprocal(rstd[0:NT, :], std[0:NT, :])
                    dve.drain()
                    dve.scalar_tensor_tensor(out=nmr[0:NT, :], in0=mv[0:NT, :, 0], scalar=-1.0, in1=rstd[0:NT, :],
                                             op0=ALU.mult, op1=ALU.mult).then_inc(nmr_ready, 1)

                def select(u, rel_ap):
                    dve.tensor_tensor(sel[:, :, :], iota_w[:, :].unsqueeze(1).to_broadcast([P, UT, WIN]),
                                      rel_ap.unsqueeze(2).to_broadcast([P, UT, WIN]), ALU.is_equal)
                    dve.tensor_tensor(rsel[:, :, :], iota_r[:, :].unsqueeze(1).to_broadcast([P, UT, REL]),
                                      type_t[:, bass.ds(UT * u, UT)].unsqueeze(2).to_broadcast([P, UT, REL]),
                                      ALU.is_equal).then_inc(sel_ready, 1)

                def add_counts(starts):
                    q = dve.snap(qa, min_val=1, max_val=1 << 24)
                    dve.wait_ge(cnt_mm, q)
                    dve.reg_add(qa, qa, 1)
                    for b in range(UNIT):
                        here = cnt[:, bass.ds(starts[b], WIN)]
                        dve.tensor_tensor(here, here, pcnt[0:REL, b * WIN:(b + 1) * WIN], ALU.add)
                        dve.drain()

                def supertile(s, more):
                    for t in range(SUB):
                        u = SUB * s + t
                        h = t % 2
                        select(u, rel0_t[:, bass.ds(UT * u, UT)])
                        dve.wait_ge(proj_done, u + 1)
                        dve.wait_ge(kv_acc, u + 1)
                        dve.wait_ge(e_done, u + 1)
                        dve.tensor_tensor(zk[0:NT, h, :], pproj[h][0:NT, 0:C], bkv_sb[0:NT, 0:C], ALU.add)
                        dve.tensor_tensor(vx[0:NT, h, :, 0:P],
                                          pproj[h][0:NT, C:2 * C].rearrange("p (k n) -> p k n", k=KC),
                                          bkv_sb[0:NT, C:2 * C].rearrange("p (k n) -> p k n", k=KC),
                                          ALU.add).then_inc(z_done, 1)
                        if more and t == 0:
                            statistics(s + 1)
                        if more and t == 1:
                            scales(s + 1)
                        starts = load_row(dve, base0_row[0:1, bass.ds(UNIT * u, UNIT)], 0, N)
                        nw = dve.value_load(nwu_row[0:1, bass.ds(u, 1)], min_val=1, max_val=N)
                        add_counts(starts)
                        with dve.If(nw > 1):
                            dve.memset(wofs[:, :], float(WIN))
                            dve.drain()
                            with dve.Fori(1, nw):
                                dve.tensor_scalar(basew[:, :], vmin_b[:, bass.ds(UNIT * u, UNIT)], wofs[:, 0:1],
                                                  float(N), ALU.add, ALU.min)
                                dve.drain()
                                dve.tensor_scalar(wofs[:, :], wofs[:, :], float(WIN), None, ALU.add)
                                dve.tensor_copy(base_i[:, :], basew[0:1, :])
                                dve.tensor_tensor(rel[:, :].rearrange("p (b t) -> p b t", t=BT),
                                                  dst_t[:, bass.ds(UT * u, UT)].rearrange("p (b t) -> p b t", t=BT),
                                                  basew[:, :].unsqueeze(2).to_broadcast([P, UNIT, BT]), ALU.subtract)
                                dve.drain()
                                select(u, rel[:, :])
                                add_counts(load_row(dve, base_i[0:1, :], 0, N))

                statistics(0)
                scales(0)
                dve.wait_ge(bkv_in, 32)
                with dve.Fori(0, SUPER - 1) as s:
                    supertile(s, True)
                supertile(SUPER - 1, False)
                dve.wait_ge(kv_acc, STEPS + 2)
                for k in range(KC):
                    dve.tensor_tensor(kv_bd[:, k, :], pkv[:, k * (P + 1):k * (P + 1) + P], head_mask[:, :], ALU.mult)
                    dve.tensor_scalar(ksum_bd[:, k, :], head_mask[:, :], pkv[:, k * (P + 1) + P:(k + 1) * (P + 1)],
                                      None, ALU.mult)

            @block.tensor
            def _(pe):
                pe.sem_inc(kv_acc, 2)
                pe.wait_ge(kv_zero, 1)
                pe.matmul(pkv[:, 0:2 * (P + 1)], zero[:, 0:P], zero[:, :], start=True, stop=True)
                qa = pe.alloc_register("count_passes_pe")
                pe.reg_mov(qa, 1)

                def turn(s):
                    pe.wait_ge(xn_ready, s + 1)
                    for k in range(KC):
                        for t in range(SUB):
                            last = pe.transpose(tb[k][:, t * NT:(t + 1) * NT], xn[0:NT, t, k * P:(k + 1) * P],
                                                ident[0:NT, 0:NT])
                    last.then_inc(tr_done, 1)

                def count():
                    q = pe.snap(qa, min_val=1, max_val=1 << 24)
                    pe.wait_ge(sel_ready, q)
                    pe.reg_add(qa, qa, 1)
                    for e in range(UT):
                        last = pe.matmul(pcnt[0:REL, (e // BT) * WIN:(e // BT + 1) * WIN], rsel[:, e, :],
                                         sel[:, e, :], start=(e % BT == 0), stop=(e % BT == BT - 1))
                    last.then_inc(cnt_mm, 1)

                def kv_sum(u, h):
                    pe.wait_ge(kf_done, u + 3)
                    for k in range(KC):
                        last = pe.matmul(pkv[:, k * (P + 1):(k + 1) * (P + 1)], kf[0:NT, h, k * P:(k + 1) * P],
                                         vx[0:NT, h, k, :], start=False, stop=True, skip_group_check=True)
                    last.then_inc(kv_acc, 1)

                def supertile(s, more, first):
                    for t in range(SUB):
                        u = SUB * s + t
                        if t == 0:
                            pe.wait_ge(xnt_ready, s + 1)
                        pe.wait_ge(z_done, u + 1)
                        for k in range(KC):
                            last = pe.matmul(pproj[t % 2][0:NT, :], xnt[:, t, k, :], wkv_sb[:, k, :],
                                             start=(k == 0), stop=(k == KC - 1))
                        last.then_inc(proj_done, 1)
                        if more and t == SUB - 1:
                            turn(s + 1)
                        nw = pe.value_load(nwu_row[0:1, bass.ds(u, 1)], min_val=1, max_val=N)
                        count()
                        with pe.If(nw > 1):
                            with pe.Fori(1, nw):
                                count()
                        if not (first and t == 0):
                            kv_sum(u - 1, (t - 1) % 2)

                turn(0)
                pe.wait_ge(wkv_in, 32)
                supertile(0, True, True)
                with pe.Fori(1, SUPER - 1) as s:
                    supertile(s, True, False)
                supertile(SUPER - 1, False, False)
                kv_sum(STEPS - 1, (STEPS - 1) % 2)

        pb = ExitStack()
        with pb:
            xb = sbuf(pb, "xb", [P, SUB, KC, NT])
            yst = sbuf(pb, "yst", [P, 2, REL, C])
            ty = sbuf(pb, "ty", [REL, UT * P], I32)
            rt = sbuf(pb, "rt", [REL, 2, UT * P])
            wofs = sbuf(pb, "wofs_b", [P, 1])
            basew = sbuf(pb, "basew_b", [P, UNIT])
            base_i = sbuf(pb, "base_b", [1, UNIT], I32)
            rel = sbuf(pb, "rel_b", [P, UT])
            sel = sbuf(pb, "sel_b", [P, UT, WIN])
            got = sbuf(pb, "got_b", [P, UT])
            cnt_e = sbuf(pb, "cnt_e", [P, UT])
            inv_e = sbuf(pb, "inv_e", [P, UT])
            yb = [psum(pb, f"yb{i}") for i in range(2)]
            gb = [psum(pb, f"gb{i}") for i in range(2)]

            xb_in = [sem(f"xb_in{t}") for t in range(SUB)]
            y_mm, y_ev, ty_row, rt_ready, base_ready, look_free, look_mm, unit_done = (
                sem(n) for n in ("y_mm", "y_ev", "ty_row", "rt_ready", "base_ready", "look_free", "look_mm", "unit_done"))
            y_out = [sem(f"y_out{i}") for i in range(2)]

            block = pb.enter_context(nc.Block())
            RB = REL // 2

            @block.sync
            def _(sp):
                sp.sem_inc(y_mm, SUB * RB)
                with sp.Fori(0, SUPER) as s:
                    for t in range(SUB):
                        sp.wait_ge(y_mm, RB * (SUB * s + t + 1))
                        sp.dma_start(xb[:, t, :, :].rearrange("p k n -> p (k n)"),
                                     xt_tab[bass.ds(s, 1), :, t * KC * NT:(t + 1) * KC * NT]
                                     .rearrange("a p n -> (a p) n")).then_inc(xb_in[t], 16)

            @block.scalar
            def _(act):
                for i in range(2):
                    act.sem_inc(y_out[i], 16)
                act.sem_inc(y_ev, 2)
                with act.Fori(0, SUPER) as s:
                    for t in range(SUB):
                        u = SUB * s + t
                        act.wait_ge(y_out[t % 2], 16 * (2 * s + t // 2 + 1))
                        for r in range(RB):
                            act.wait_ge(y_mm, SUB * RB + RB * u + r + 1)
                            act.activation(yst[0:NT, t % 2, 2 * r:2 * r + 2, :],
                                           yb[r % 2][0:NT, :].rearrange("p (r n) -> p r n", r=2),
                                           ACT.Copy).then_inc(y_ev, 1)
                        act.wait_ge(y_ev, RB * (u + 1) + 2)
                        act.dma_start(y_tab.rearrange("(r n) c -> n r c", r=REL)[bass.ds(u * NT, NT), :, :],
                                      yst[0:NT, t % 2, :, :]).then_inc(y_out[t % 2], 16)
                for i in range(2):
                    act.wait_ge(y_out[i], 16 * (STEPS // 2 + 1))

            @block.gpsimd
            def _(pool):
                units = pool.alloc_register("type_units")
                read = pool.alloc_register("type_reads")
                for r in (units, read):
                    pool.reg_mov(r, 1)
                with pool.Fori(0, SUPER) as s:
                    for t in range(SUB):
                        u = SUB * s + t
                        pool.dma_start(ty[:, :], ty_tab[bass.ds(u * UT * P, UT * P)]
                                       .rearrange("(a n) -> a n", a=1).to_broadcast([REL, UT * P])).then_inc(ty_row, 16)
                        n = pool.snap(units, min_val=1, max_val=STEPS)
                        pool.wait_ge(ty_row, 16 * (u + 1))
                        pool.wait_ge(unit_done, n)
                        pool.reg_add(units, units, 1)
                        pool.tensor_scalar(rt[:, t % 2, :], ty[:, :], iota_p[:, 0:1], None, ALU.is_equal
                                           ).then_inc(rt_ready, 1)
                        m = pool.snap(read, min_val=1, max_val=STEPS)
                        pool.wait_ge(rt_ready, m)
                        pool.reg_add(read, read, 1)

            @block.vector
            def _(dve):
                dve.sem_inc(unit_done, 2)
                dve.sem_inc(look_free, 1)
                qb = dve.alloc_register("look_passes")
                dve.reg_mov(qb, 1)

                def select(rel_ap):
                    dve.tensor_tensor(sel[:, :, :], iota_w[:, :].unsqueeze(1).to_broadcast([P, UT, WIN]),
                                      rel_ap.unsqueeze(2).to_broadcast([P, UT, WIN]), ALU.is_equal)
                    dve.drain()

                def look(into):
                    q = dve.snap(qb, min_val=1, max_val=1 << 24)
                    dve.wait_ge(look_mm, q)
                    dve.reg_add(qb, qb, 1)
                    H = UT // 2
                    for i in range(2):
                        last = dve.tensor_tensor(sel[:, i * H:(i + 1) * H, :], sel[:, i * H:(i + 1) * H, :],
                                                 gb[i][:, :].rearrange("p (e w) -> p e w", w=WIN), ALU.mult)
                    last.then_inc(look_free, 1)
                    dve.drain()
                    dve.tensor_reduce(into[:, :], sel[:, :, :], AX.X, ALU.add)
                    dve.drain()

                with dve.Fori(0, SUPER) as s:
                    for t in range(SUB):
                        u = SUB * s + t
                        nw = dve.value_load(nwu_row[0:1, bass.ds(u, 1)], min_val=1, max_val=N)
                        select(rel0_t[:, bass.ds(UT * u, UT)])
                        look(cnt_e)
                        with dve.If(nw > 1):
                            dve.memset(wofs[:, :], float(WIN))
                            dve.drain()
                            with dve.Fori(1, nw):
                                dve.tensor_scalar(basew[:, :], vmin_b[:, bass.ds(UNIT * u, UNIT)], wofs[:, 0:1],
                                                  float(N), ALU.add, ALU.min)
                                dve.drain()
                                dve.tensor_scalar(wofs[:, :], wofs[:, :], float(WIN), None, ALU.add)
                                dve.tensor_copy(base_i[:, :], basew[0:1, :]).then_inc(base_ready, 1)
                                dve.tensor_tensor(rel[:, :].rearrange("p (b t) -> p b t", t=BT),
                                                  dst_t[:, bass.ds(UT * u, UT)].rearrange("p (b t) -> p b t", t=BT),
                                                  basew[:, :].unsqueeze(2).to_broadcast([P, UNIT, BT]), ALU.subtract)
                                dve.drain()
                                select(rel[:, :])
                                look(got)
                                dve.tensor_tensor(cnt_e[:, :], cnt_e[:, :], got[:, :], ALU.add)
                                dve.drain()
                        dve.tensor_scalar(inv_e[:, :], cnt_e[:, :], 1.0, None, ALU.max)
                        dve.drain()
                        dve.reciprocal(inv_e[:, :], inv_e[:, :])
                        dve.drain()
                        dve.tensor_tensor(coef_t[:, bass.ds(UT * u, UT)], wt_t[:, bass.ds(UT * u, UT)], inv_e[:, :],
                                          ALU.mult).then_inc(unit_done, 1)

            @block.tensor
            def _(pe):
                qb = pe.alloc_register("look_passes_pe")
                qx = pe.alloc_register("further_passes_pe")
                for r in (qb, qx):
                    pe.reg_mov(r, 1)

                def look(t, starts):
                    q = pe.snap(qb, min_val=1, max_val=1 << 24)
                    pe.wait_ge(look_free, q)
                    pe.reg_add(qb, qb, 1)
                    for e in range(UT):
                        last = pe.matmul(gb[e // 8][:, (e % 8) * WIN:(e % 8 + 1) * WIN],
                                         rt[:, t % 2, e * P:(e + 1) * P],
                                         cnt[:, bass.ds(starts[e // BT], WIN)], start=True, stop=True)
                    last.then_inc(look_mm, 1)

                with pe.Fori(0, SUPER) as s:
                    for t in range(SUB):
                        u = SUB * s + t
                        pe.wait_ge(xb_in[t], 16 * (s + 1))
                        for r in range(RB):
                            if r == RB - 1:
                                pe.wait_ge(rt_ready, u + 1)
                            pe.wait_ge(y_ev, RB * u + r + 1)
                            for k in range(KC):
                                last = pe.matmul(yb[r % 2][0:NT, :], xb[:, t, k, :],
                                                 wrel_sb[:, k, 2 * r:2 * r + 2, :], start=(k == 0), stop=(k == KC - 1))
                            last.then_inc(y_mm, 1)
                        nw = pe.value_load(nwu_row[0:1, bass.ds(u, 1)], min_val=1, max_val=N)
                        look(t, load_row(pe, base0_row[0:1, bass.ds(UNIT * u, UNIT)], 0, N))
                        with pe.If(nw > 1):
                            with pe.Fori(1, nw):
                                f = pe.snap(qx, min_val=1, max_val=1 << 24)
                                pe.wait_ge(base_ready, f)
                                pe.reg_add(qx, qx, 1)
                                look(t, load_row(pe, base_i[0:1, :], 0, N))
        early.close()
        pc = ExitStack()
        with pc:
            xc = sbuf(pc, "xc", [P, SUB, KC, NT])
            xr = sbuf(pc, "xr", [P, SUB, C])
            eq = sbuf(pc, "eq", [P, KC, NS])
            rq = sbuf(pc, "rq", [P, KC, NS])
            qf = sbuf(pc, "qf", [P, KC, NS])
            den = sbuf(pc, "den", [P, KC, NS])
            att = sbuf(pc, "att", [P, KC, NS])
            res_t = sbuf(pc, "res_t", [P, KC, NS])
            x1 = sbuf(pc, "x1", [P, SUB, C])
            stats = sbuf(pc, "stats_c", [P, SUB, 6])
            mv = sbuf(pc, "mv_c", [P, SUB, 2])
            std = sbuf(pc, "std_c", [P, SUB])
            rstd = sbuf(pc, "rstd_c", [P, SUB])
            xn = sbuf(pc, "xn_c", [P, SUB, C])
            ft = sbuf(pc, "ft", [P, KC, NS])
            rh = sbuf(pc, "rh", [P, NS])
            h1 = sbuf(pc, "h1", [P, 2, KC, NS])
            h2 = sbuf(pc, "h2", [P, 2, KC, NS])
            y = sbuf(pc, "y", [P, SUB, C])
            lg = sbuf(pc, "lg", [P, SUB, EXPERTS])
            lmax = sbuf(pc, "lmax", [P, SUB])
            ex = sbuf(pc, "ex", [P, SUB, EXPERTS])
            esum = sbuf(pc, "esum", [P, SUB])
            probs = sbuf(pc, "probs", [P, SUB, 8])
            top = sbuf(pc, "top", [P, SUB, 8])
            top_i = sbuf(pc, "top_i", [P, SUB, 8], mybir.dt.uint32)
            top_f = sbuf(pc, "top_f", [P, SUB, 2])
            gap = sbuf(pc, "gap", [P, SUB])
            rw = sbuf(pc, "rw", [P, 2, SUB])
            hot = sbuf(pc, "hot", [P, 2, SUB, 8])
            gate = sbuf(pc, "gate", [P, SUB, 8])
            gate_t = sbuf(pc, "gate_t", [8, NS])
            ring = sbuf(pc, "ring", [P, SLOTS, BT, C])
            ring_i = sbuf(pc, "ring_i", [P, SLOTS, BT], I32)
            sc = sbuf(pc, "sc", [P, SLOTS, BT, WIN])
            first_w = sbuf(pc, "first_w", [P, BLOCKS])
            s_lo = sbuf(pc, "s_lo", [P, 1])
            s_top = sbuf(pc, "s_top", [P, 1])
            wofs = sbuf(pc, "wofs_c", [P, 1])
            thr = sbuf(pc, "thr", [P, 1])
            bw = sbuf(pc, "bw", [P, 1])
            cm = sbuf(pc, "cm", [P, BT])
            rel = sbuf(pc, "rel_c", [P, BT])
            col_i = sbuf(pc, "col_i", [1, SLOTS], I32)
            acc = [psum(pc, f"acc{k}") for k in range(KC)]
            NBANK = 6
            bank = [psum(pc, f"bank{i}") for i in range(NBANK)]

            items = [("q", m, "act") for m in range(KC)]
            for k in range(KC):
                items += [("den", k, "act"), ("num", k, "dve")]
            items += [("x1", i, "dve") for i in range(2)] + [("ft", k, "act") for k in range(KC)]
            items += [("rh", 0, "act")]
            items += [("h1", (0, m), "act") for m in range(KC)] + [("lg", 0, "dve")]
            for e in range(1, EXPERTS + 2):
                if e < EXPERTS:
                    items += [("h1", (e, m), "act") for m in range(KC)]
                if e == 2:
                    items += [("gt", 0, "act")]
                if e - 1 < EXPERTS:
                    items += [("h2", (e - 1, m), "act") for m in range(KC)]
                if e == 2:
                    items += [("b3", i, "dve") for i in range(2)]
                if e >= 2:
                    items += [("w3", (e - 2, i), "dve") for i in range(2)]
            place, nth = {}, {"act": 0, "dve": 0}
            for i, (kind, arg, eng) in enumerate(items):
                nth[eng] += 1
                place[kind, arg] = (i, eng, nth[eng])
            M = len(items)

            items_full = sem("items_full")
            emptied = {"act": sem("act_emptied"), "dve": sem("dve_emptied")}
            qf_ready, acc_full, res_act, res_dve = (sem(n) for n in ("qf_ready", "acc_full", "res_act", "res_dve"))
            var_c, std_c, xn_c, d_ready, ex_ready, gap_ready, g2_ready, gate_ready = (
                sem(n) for n in ("var_c", "std_c", "xn_c", "d_ready", "ex_ready", "gap_ready", "g2_ready", "gate_ready"))
            y_ready, y_stored, xc_in, xr_in = (sem(n) for n in ("y_ready", "y_stored", "xc_in", "xr_in"))
            idx_ready, sc_ready = sem("idx_ready"), sem("sc_ready")
            rows_in = [sem(f"rows_in{j}") for j in range(SLOTS)]
            slot_used = [sem(f"slot_used{j}") for j in range(SLOTS)]

            def full(s, kind, arg):
                return (s + 1) * M + place[kind, arg][0] + 1

            def done(s, kind, arg):
                _, eng, c = place[kind, arg]
                return emptied[eng], (s + 1) * nth[eng] + c

            def bank_of(kind, arg):
                return bank[place[kind, arg][0] % NBANK]

            block = pc.enter_context(nc.Block())

            def slots_of(eng, s, body):
                lo = eng.value_load(lo_row[0:1, bass.ds(s, 1)], min_val=0, max_val=BLOCKS - 1)
                hi = eng.value_load(hi_row[0:1, bass.ds(s, 1)], min_val=1, max_val=BLOCKS)
                with eng.Fori(0, (hi - lo + (SLOTS - 1)) // SLOTS) as i:
                    for j in range(SLOTS):
                        blk = eng.snap(lo + i * SLOTS + j, min_val=0, max_val=BLOCKS + SLOTS)
                        with eng.If(blk < hi):
                            body(j, blk.with_bounds(min_val=0, max_val=BLOCKS - 1))

            @block.sync
            def _(sp):
                def load_xc(s):
                    sp.dma_start(xc[:, :, :, :].rearrange("p t k n -> p (t k n)"),
                                 xt_tab[bass.ds(s, 1), :, :].rearrange("a p n -> (a p) n")).then_inc(xc_in, 16)

                def load_xr(s):
                    sp.dma_start(xr[0:NT, :, :], x[bass.ds(s * NS, NS), :].rearrange("(t p) c -> p t c", p=NT)
                                 ).then_inc(xr_in, 16)

                def store(s):
                    sp.wait_ge(y_ready, s + 1)
                    sp.dma_start(out[bass.ds(s * NS, NS), :].rearrange("(t p) c -> p t c", p=NT),
                                 y[0:NT, :, :]).then_inc(y_stored, 16)

                sp.sem_inc(y_stored, 16)
                load_xc(0)
                load_xr(0)
                with sp.Fori(0, SUPER - 1) as s:
                    sp.wait_ge(items_full, full(s, "den", 0))
                    load_xc(s + 1)
                    sp.wait_ge(*done(s, "x1", 1))
                    load_xr(s + 1)
                    store(s)
                store(SUPER - 1)
                sp.wait_ge(y_stored, 16 * (SUPER + 1))

            @block.gpsimd
            def _(pool):
                uses = [pool.alloc_register(f"slot_uses{j}") for j in range(SLOTS)]
                copies = pool.alloc_register("idx_copies")
                for r in uses + [copies]:
                    pool.reg_mov(r, 1)
                with pool.Fori(0, SUPER) as s:
                    def gather(j, blk):
                        nw = pool.value_load(nwin_row[0:1, bass.ds(blk, 1)], min_val=1, max_val=MAXW)
                        used = pool.snap(uses[j], min_val=1, max_val=1 << 24)
                        pool.wait_ge(slot_used[j], used)
                        pool.reg_add(uses[j], uses[j], nw)
                        pool.tensor_copy(ring_i[:, j, :], idx_t[:, bass.ds(blk * BT, BT)]).then_inc(idx_ready, 1)
                        copied = pool.snap(copies, min_val=1, max_val=1 << 24)
                        pool.wait_ge(idx_ready, copied)
                        pool.reg_add(copies, copies, 1)
                        for q in range(BT):
                            pool.indirect_dma_start(
                                out=ring[:, j, q, :], out_offset=None, in_=y_tab[:, :],
                                in_offset=bass.IndirectOffsetOnAxis(ap=ring_i[:, j, q:q + 1], axis=0),
                            ).then_inc(rows_in[j], 16)
                    slots_of(pool, s, gather)

            @block.scalar
            def _(act):
                act.sem_inc(emptied["act"], nth["act"])
                with act.Fori(0, SUPER) as s:
                    def take(kind, arg):
                        act.wait_ge(items_full, full(s, kind, arg))
                        return bank_of(kind, arg)

                    def gone(last):
                        last.then_inc(emptied["act"], 1)

                    def hidden(kind, e, m):
                        b = take(kind, (e, m))
                        dest, row = (h1, EB1) if kind == "h1" else (h2, EB2)
                        gone(act.activation(dest[:, e % 2, m, :], b[:, 0:NS], ACT.Relu,
                                            bias=bias_t[:, row + KC * e + m:row + KC * e + m + 1]))

                    for m in range(KC):
                        b = take("q", m)
                        act.activation(eq[:, m, :], b[:, 0:NS], ACT.Exp, bias=bias_t[:, BQ + m:BQ + m + 1])
                        gone(act.activation(rq[:, m, :], b[:, 0:NS], ACT.Relu, bias=bias_t[:, BQ + m:BQ + m + 1]))
                    for k in range(KC):
                        b = take("den", k)
                        gone(act.activation(den[:, k, :], b[:, 0:NS], ACT.Identity, bias=eps_den[:, :]))
                    act.wait_ge(acc_full, s + 1)
                    act.activation(res_t[:, 0, :], acc[0][:, 0:NS], ACT.Identity, bias=out_bias[:, 0:1]
                                   ).then_inc(res_act, 1)
                    act.wait_ge(var_c, s + 1)
                    act.activation(std[0:NT, :], mv[0:NT, :, 1], ACT.Sqrt, bias=eps_ln[0:NT, :]).then_inc(std_c, 1)
                    for k in range(KC):
                        b = take("ft", k)
                        gone(act.activation(ft[:, k, :], b[:, 0:NS], ACT.Copy))
                    b = take("rh", 0)
                    gone(act.activation(rh[:, :], b[:, 0:NS], ACT.Relu, bias=bias_t[:, RB1:RB1 + 1]))
                    for m in range(KC):
                        hidden("h1", 0, m)
                    for e in range(1, EXPERTS + 1):
                        if e < EXPERTS:
                            for m in range(KC):
                                hidden("h1", e, m)
                                if e == 1 and m == 0:
                                    act.wait_ge(d_ready, s + 1)
                                    act.activation(ex[0:NT, :, :], lg[0:NT, :, :], ACT.Exp).then_inc(ex_ready, 1)
                        if e == 2:
                            gone(act.activation(gate_t[:, :], take("gt", 0)[0:8, 0:NS], ACT.Copy))
                        for m in range(KC):
                            hidden("h2", e - 1, m)
                            if e == 1 and m == 0:
                                act.wait_ge(gap_ready, s + 1)
                                act.activation(rw[0:NT, 1, :], gap[0:NT, :], ACT.Exp).then_inc(g2_ready, 1)

            @block.vector
            def _(dve):
                dve.sem_inc(emptied["dve"], nth["dve"])
                uses = [dve.alloc_register(f"slot_uses_dve{j}") for j in range(SLOTS)]
                for r in uses:
                    dve.reg_mov(r, 1)
                dve.memset(probs[:, :, :], -1.0)
                dve.memset(s_lo[:, :], 0.0)
                dve.memset(s_top[:, :], float(NS - WIN))
                dve.drain()
                with dve.Fori(0, SUPER) as s:
                    def take(kind, arg):
                        dve.wait_ge(items_full, full(s, kind, arg))
                        return bank_of(kind, arg)

                    def gone(last):
                        last.then_inc(emptied["dve"], 1)

                    for k in range(KC):
                        dve.wait_ge(*done(s, "q", k))
                        dve.scalar_tensor_tensor(out=qf[:, k, :], in0=eq[:, k, :], scalar=1.0, in1=rq[:, k, :],
                                                 op0=ALU.min, op1=ALU.add).then_inc(qf_ready, 1)
                    for k in range(KC):
                        dve.wait_ge(*done(s, "den", k))
                        dve.reciprocal(den[:, k, :], den[:, k, :])
                        dve.drain()
                        b = take("num", k)
                        gone(dve.tensor_tensor(att[:, k, :], b[:, 0:NS], den[:, k, :], ALU.mult))

                    dve.tensor_scalar(first_w[:, :], vmin_b[:, :], s_lo[:, 0:1], s_top[:, 0:1], ALU.max, ALU.min)
                    dve.drain()

                    def windows(j, blk):
                        nw = dve.value_load(nwin_row[0:1, bass.ds(blk, 1)], min_val=1, max_val=MAXW)
                        dve.memset(wofs[:, :], 0.0)
                        dve.drain()
                        with dve.Fori(0, nw):
                            dve.tensor_scalar(thr[:, :], first_w[:, bass.ds(blk, 1)], wofs[:, 0:1], None, ALU.add)
                            dve.tensor_scalar(bw[:, :], first_w[:, bass.ds(blk, 1)], wofs[:, 0:1], s_top[:, 0:1],
                                              ALU.add, ALU.min)
                            dve.drain()
                            dve.tensor_scalar(wofs[:, :], wofs[:, :], float(WIN), None, ALU.add)
                            dve.scalar_tensor_tensor(out=cm[:, :], in0=dst_t[:, bass.ds(blk * BT, BT)],
                                                     scalar=thr[:, 0:1], in1=coef_t[:, bass.ds(blk * BT, BT)],
                                                     op0=ALU.is_ge, op1=ALU.mult)
                            dve.tensor_scalar(rel[:, :], dst_t[:, bass.ds(blk * BT, BT)], bw[:, 0:1], None,
                                              ALU.subtract)
                            dve.wait_ge(slot_used[j], dve.snap(uses[j], min_val=1, max_val=1 << 24))
                            dve.tensor_scalar(col_i[0:1, j:j + 1], bw[0:1, :], s_lo[0:1, 0:1], None, ALU.subtract)
                            dve.drain()
                            for q in range(BT):
                                last = dve.tensor_scalar(sc[:, j, q, :], iota_w[:, :], rel[:, q:q + 1], cm[:, q:q + 1],
                                                         ALU.is_equal, ALU.mult)
                            last.then_inc(sc_ready, 1)
                            dve.drain()
                            dve.reg_add(uses[j], uses[j], 1)
                    slots_of(dve, s, windows)
                    dve.tensor_scalar(s_lo[:, :], s_lo[:, :], float(NS), None, ALU.add)
                    dve.tensor_scalar(s_top[:, :], s_top[:, :], float(NS), None, ALU.add)

                    dve.wait_ge(acc_full, s + 1)
                    dve.tensor_scalar(res_t[:, 1, :], acc[1][:, 0:NS], out_bias[:, 1:2], None, ALU.add
                                      ).then_inc(res_dve, 1)
                    dve.wait_ge(xr_in, 16 * (s + 1))
                    for i in range(2):
                        b = take("x1", i)
                        gone(dve.tensor_tensor(x1[0:NT, 2 * i:2 * i + 2, :],
                                               b[0:NT, :].rearrange("p (t c) -> p t c", t=2),
                                               xr[0:NT, 2 * i:2 * i + 2, :], ALU.add))
                    dve.drain()
                    for t in range(SUB):
                        dve.bn_stats(stats[0:NT, t, :], x1[0:NT, t, :])
                    dve.drain()
                    for t in range(SUB):
                        last = dve.bn_aggr(mv[0:NT, t, :], stats[0:NT, t, :])
                    last.then_inc(var_c, 1)
                    dve.wait_ge(std_c, s + 1)
                    dve.reciprocal(rstd[0:NT, :], std[0:NT, :])
                    dve.drain()
                    for t in range(SUB):
                        last = dve.tensor_scalar(xn[0:NT, t, :], x1[0:NT, t, :], mv[0:NT, t, 0:1], rstd[0:NT, t:t + 1],
                                                 ALU.subtract, ALU.mult)
                    last.then_inc(xn_c, 1)

                    def by_expert(v, n):
                        return v.unsqueeze(2).to_broadcast([NT, SUB, n])
                    b = take("lg", 0)
                    gone(dve.tensor_tensor(lg[0:NT, :, :],
                                           b[0:NT, 0:SUB * EXPERTS].rearrange("p (t e) -> p t e", t=SUB),
                                           rb2_sb[0:NT, :].unsqueeze(1).to_broadcast([NT, SUB, EXPERTS]), ALU.add))
                    dve.drain()
                    dve.tensor_reduce(lmax[0:NT, :], lg[0:NT, :, :], AX.X, ALU.max)
                    dve.drain()
                    dve.tensor_tensor(lg[0:NT, :, :], lg[0:NT, :, :], by_expert(lmax[0:NT, :], EXPERTS),
                                      ALU.subtract).then_inc(d_ready, 1)
                    dve.wait_ge(ex_ready, s + 1)
                    dve.tensor_reduce(esum[0:NT, :], ex[0:NT, :, :], AX.X, ALU.add)
                    dve.drain()
                    dve.reciprocal(esum[0:NT, :], esum[0:NT, :])
                    dve.drain()
                    dve.tensor_tensor(probs[0:NT, :, 0:EXPERTS], ex[0:NT, :, :], by_expert(esum[0:NT, :], EXPERTS),
                                      ALU.mult)
                    dve.drain()
                    for t in range(SUB):
                        dve.max(top[0:NT, t, :], probs[0:NT, t, :])
                    dve.drain()
                    dve.tensor_tensor(gap[0:NT, :], top[0:NT, :, 1], top[0:NT, :, 0], ALU.subtract
                                      ).then_inc(gap_ready, 1)
                    for t in range(SUB):
                        dve.max_index(top_i[0:NT, t, :], top[0:NT, t, :], probs[0:NT, t, :])
                    dve.drain()
                    dve.tensor_copy(top_f[0:NT, :, :], top_i[0:NT, :, 0:2])
                    dve.wait_ge(g2_ready, s + 1)
                    dve.tensor_scalar(rw[0:NT, 0, :], rw[0:NT, 1, :], 1.0, None, ALU.add)
                    dve.drain()
                    dve.reciprocal(rw[0:NT, 0, :], rw[0:NT, 0, :])
                    dve.drain()
                    dve.tensor_tensor(rw[0:NT, 1, :], rw[0:NT, 1, :], rw[0:NT, 0, :], ALU.mult)
                    for i in range(2):
                        dve.tensor_tensor(hot[0:NT, i, :, :],
                                          iota_w[0:NT, 0:8].unsqueeze(1).to_broadcast([NT, SUB, 8]),
                                          by_expert(top_f[0:NT, :, i], 8), ALU.is_equal)
                    dve.drain()
                    for i in range(2):
                        dve.tensor_tensor(hot[0:NT, i, :, :], hot[0:NT, i, :, :], by_expert(rw[0:NT, i, :], 8), ALU.mult)
                    dve.drain()
                    dve.tensor_tensor(gate[0:NT, :, :], hot[0:NT, 0, :, :], hot[0:NT, 1, :, :], ALU.add
                                      ).then_inc(gate_ready, 1)
                    dve.wait_ge(y_stored, 16 * (s + 1))
                    for i in range(2):
                        b = take("b3", i)
                        gone(dve.tensor_tensor(y[0:NT, 2 * i:2 * i + 2, :],
                                               b[0:NT, :].rearrange("p (t c) -> p t c", t=2),
                                               x1[0:NT, 2 * i:2 * i + 2, :], ALU.add))
                    for e in range(EXPERTS):
                        dve.drain()
                        for i in range(2):
                            b = take("w3", (e, i))
                            for t in (2 * i, 2 * i + 1):
                                last = dve.scalar_tensor_tensor(out=y[0:NT, t, :], in0=b[0:NT, (t % 2) * C:(t % 2 + 1) * C],
                                                                scalar=gate[0:NT, t, e:e + 1], in1=y[0:NT, t, :],
                                                                op0=ALU.mult, op1=ALU.add)
                            gone(last)
                    dve.drain()
                    dve.sem_inc(y_ready, 1)

            @block.tensor
            def _(pe):
                pe.sem_inc(items_full, M)
                for j in range(SLOTS):
                    pe.sem_inc(slot_used[j], 1)
                uses = [pe.alloc_register(f"slot_rows_pe{j}") for j in range(SLOTS)]
                passes = pe.alloc_register("passes_pe")
                for r in uses:
                    pe.reg_mov(r, 16 * BT)
                pe.reg_mov(passes, 1)
                with pe.Fori(0, SUPER) as s:
                    def give(kind, arg):
                        i = place[kind, arg][0]
                        last = max([n for n in range(i) if n % NBANK == i % NBANK], default=None)
                        if last is None:
                            last = max(n for n in range(M) if n % NBANK == i % NBANK)
                            sem_, v = done(s - 1, *items[last][:2])
                        else:
                            sem_, v = done(s, *items[last][:2])
                        pe.wait_ge(sem_, v)
                        return bank[i % NBANK]

                    def filled(last):
                        last.then_inc(items_full, 1)

                    def by_sub(b):
                        return b[:, 0:NS].rearrange("p (t n) -> p t n", t=SUB)

                    def hidden(kind, e, m):
                        w, src_t = (w1_sb, ft) if kind == "h1" else (w2_sb, h1[:, e % 2, :, :])
                        b = give(kind, (e, m))
                        if kind == "h2":
                            pe.wait_ge(*done(s, "h1", (e, KC - 1)))
                        for k in range(KC):
                            last = pe.matmul(b[:, 0:NS], w[:, e, k, m * P:(m + 1) * P], src_t[:, k, :],
                                             start=(k == 0), stop=(k == KC - 1))
                        filled(last)

                    pe.wait_ge(xc_in, 16 * (s + 1))
                    for m in range(KC):
                        b = give("q", m)
                        for k in range(KC):
                            last = pe.matmul(by_sub(b), wq_sb[:, k, m * P:(m + 1) * P], xc[:, :, k, :],
                                             start=(k == 0), stop=(k == KC - 1))
                        filled(last)
                    for m in range(KC):
                        for k in range(KC):
                            pe.matmul(by_sub(acc[m]), root_sb[:, k, m * P:(m + 1) * P], xc[:, :, k, :],
                                      start=(k == 0), stop=False, skip_group_check=True)
                    for k in range(KC):
                        b = give("den", k)
                        pe.wait_ge(qf_ready, KC * s + k + 1)
                        filled(pe.matmul(b[:, 0:NS], ksum_bd[:, k, :], qf[:, k, :], start=True, stop=True))
                        b = give("num", k)
                        filled(pe.matmul(b[:, 0:NS], kv_bd[:, k, :], qf[:, k, :], start=True, stop=True))

                    def aggregate(j, blk):
                        nw = pe.value_load(nwin_row[0:1, bass.ds(blk, 1)], min_val=1, max_val=MAXW)
                        arrived = pe.snap(uses[j], min_val=1, max_val=1 << 24)
                        pe.wait_ge(rows_in[j], arrived)
                        pe.reg_add(uses[j], uses[j], 16 * BT)
                        with pe.Fori(0, nw):
                            built = pe.snap(passes, min_val=1, max_val=1 << 24)
                            pe.wait_ge(sc_ready, built)
                            pe.reg_add(passes, passes, 1)
                            col = pe.value_load(col_i[0:1, j:j + 1], min_val=0, max_val=NS - WIN)
                            for q in range(BT):
                                for k in range(KC):
                                    last = pe.matmul(acc[k][:, bass.ds(col, WIN)], ring[:, j, q, k * P:(k + 1) * P],
                                                     sc[:, j, q, :], start=False, stop=False, skip_group_check=True)
                            last.then_inc(slot_used[j], 1)
                    slots_of(pe, s, aggregate)

                    pe.wait_ge(*done(s, "num", KC - 1))
                    for m in range(KC):
                        for k in range(KC):
                            last = pe.matmul(acc[m][:, 0:NS], wo_sb[:, k, m * P:(m + 1) * P], att[:, k, :],
                                             start=False, stop=(k == KC - 1), skip_group_check=True)
                    last.then_inc(acc_full, 1)
                    pe.wait_ge(res_act, s + 1)
                    pe.wait_ge(res_dve, s + 1)
                    for i in range(2):
                        b = give("x1", i)
                        for t in (2 * i, 2 * i + 1):
                            for k in range(KC):
                                o = (t % 2) * C + k * P
                                last = pe.transpose(b[0:NT, o:o + P], res_t[:, k, t * NT:(t + 1) * NT], ident[:, :])
                        filled(last)
                    for k in range(KC):
                        b = give("ft", k)
                        pe.wait_ge(xn_c, s + 1)
                        for t in range(SUB):
                            last = pe.transpose(b[:, t * NT:(t + 1) * NT], xn[0:NT, t, k * P:(k + 1) * P],
                                                ident[0:NT, 0:NT])
                        filled(last)
                    b = give("rh", 0)
                    pe.wait_ge(*done(s, "ft", KC - 1))
                    for k in range(KC):
                        last = pe.matmul(b[:, 0:NS], rw1_sb[:, k, :], ft[:, k, :], start=(k == 0), stop=(k == KC - 1))
                    filled(last)
                    for m in range(KC):
                        hidden("h1", 0, m)
                    b = give("lg", 0)
                    pe.wait_ge(*done(s, "rh", 0))
                    for t in range(SUB):
                        last = pe.matmul(b[0:NT, t * EXPERTS:(t + 1) * EXPERTS], rh[:, t * NT:(t + 1) * NT],
                                         rw2_sb[:, :], start=True, stop=True)
                    filled(last)
                    for e in range(1, EXPERTS + 2):
                        if e < EXPERTS:
                            for m in range(KC):
                                hidden("h1", e, m)
                        if e == 2:
                            b = give("gt", 0)
                            pe.wait_ge(gate_ready, s + 1)
                            for t in range(SUB):
                                last = pe.transpose(b[0:8, t * NT:(t + 1) * NT], gate[0:NT, t, :], ident[0:NT, 0:NT])
                            filled(last)
                        if e - 1 < EXPERTS:
                            for m in range(KC):
                                hidden("h2", e - 1, m)
                        if e == 2:
                            pe.wait_ge(*done(s, "gt", 0))
                            for i in range(2):
                                b = give("b3", i)
                                for t in (2 * i, 2 * i + 1):
                                    last = pe.matmul(b[0:NT, (t % 2) * C:(t % 2 + 1) * C],
                                                     gate_t[0:EXPERTS, t * NT:(t + 1) * NT], b3_sb[:, :],
                                                     start=True, stop=True)
                                filled(last)
                        if e >= 2:
                            pe.wait_ge(*done(s, "h2", (e - 2, KC - 1)))
                            for i in range(2):
                                b = give("w3", (e - 2, i))
                                for t in (2 * i, 2 * i + 1):
                                    for k in range(KC):
                                        last = pe.matmul(b[0:NT, (t % 2) * C:(t % 2 + 1) * C],
                                                         h2[:, e % 2, k, t * NT:(t + 1) * NT], w3_sb[:, e - 2, k, :],
                                                         start=(k == 0), stop=(k == KC - 1))
                                filled(last)


_INS = ["x", "src", "dst", "edge_type_8", "edge_weight", "L0_gnn_weight", "L0_gnn_root", "L0_gnn_bias",
        "L0_mix_wq", "L0_mix_bq", "L0_mix_wk", "L0_mix_bk", "L0_mix_wv", "L0_mix_bv", "L0_mix_wo", "L0_mix_bo",
        "L0_ffn_router_w1", "L0_ffn_router_b1", "L0_ffn_router_w2", "L0_ffn_router_b2",
        "L0_ffn_expert_w1", "L0_ffn_expert_b1", "L0_ffn_expert_w2", "L0_ffn_expert_b2",
        "L0_ffn_expert_w3", "L0_ffn_expert_b3"]


def kernel(**inputs):
    import numpy as _np
    import concourse.bacc as _bacc
    from concourse import mybir as _mybir
    from concourse.bass_utils import run_bass_kernel_spmd as _run

    nc = _bacc.Bacc("TRN2", target_bir_lowering=False, num_devices=1)
    arrays, args = {}, []
    for name in _INS:
        a = _np.ascontiguousarray(inputs[name])
        arrays[f"in_{name}"] = a
        args.append(nc.dram_tensor(f"in_{name}", a.shape, _mybir.dt.from_np(a.dtype), kind="ExternalInput").ap())
    args.append(nc.dram_tensor("out_0", (12500, 256), _mybir.dt.float32, kind="ExternalOutput").ap())
    gps_layer(nc, *args)
    r = _run(nc, [arrays], core_ids=[0])
    return r.results[0]["out_0"]
```

```python
import concourse.bass as bass
from concourse import mybir
from concourse.alu_op_type import AluOpType as ALU
from contextlib import ExitStack

F32 = mybir.dt.float32
F32R = mybir.dt.float32r
BF16 = mybir.dt.bfloat16
I32 = mybir.dt.int32
ACT = mybir.ActivationFunctionType
AX = mybir.AxisListType

N, C, E, REL = 12500, 256, 200000, 8
HEADS, EXPERTS = 8, 6
P = 128
KC = C // P
SUPER = 25
NS = N // SUPER
SUB = 4
NT = NS // SUB
STEPS = SUPER * SUB
BT = 4
BE = BT * P
REAL_BLOCKS = -(-E // BE)
UNIT = 4
BLOCKS = STEPS * UNIT
TILES = BLOCKS * BT
UT = UNIT * BT
WIN = 64
MAXW = -(-NS // WIN)
CHUNK = 3
CT = CHUNK * BT
GROUPS = 3
RANGE = EXPERTS * CHUNK
NP = 512
DIGITS = 3
DR = DIGITS * REL
LN_EPS = 1e-5
DEN_EPS = 1e-6


def gps_layer(nc, x, src, dst, etype, ew, g_w, g_root, g_b, wq, bq, wk, bk, wv, bv, wo, bo,
              r_w1, r_b1, r_w2, r_b2, e_w1, e_b1, e_w2, e_b2, e_w3, e_b3, out):
    assert BLOCKS >= REAL_BLOCKS and N == SUPER * SUB * NT
    y_tab = nc.dram_tensor("y_tab", [REL * N, C], F32).ap()
    xt_tab = nc.dram_tensor("xt_tab", [SUPER, P, KC * NP], F32).ap()
    ty_tab = nc.dram_tensor("ty_tab", [BLOCKS * BE], I32).ap()

    def load_row(eng, row, least, most):
        _, values = nc.values_load_multi_w_load_instructions(row, engines=(eng.engine,), min_val=least, max_val=most)
        return values

    whole = ExitStack()
    with whole:
        def sbuf(scope, name, shape, dt=F32):
            return scope.enter_context(nc.sbuf_tensor(name, shape, dt))

        def psum(scope, name, shape=(P, 512)):
            return scope.enter_context(nc.psum_tensor(name, list(shape), F32))

        def sem(name):
            return whole.enter_context(nc.semaphore(name))

        w2_sb = sbuf(whole, "w2_sb", [P, EXPERTS, KC, C])
        w3_sb = sbuf(whole, "w3_sb", [P, EXPERTS, KC, C])
        wq_sb = sbuf(whole, "wq_sb", [P, KC, C])
        wo_sb = sbuf(whole, "wo_sb", [P, KC, C])
        root_sb = sbuf(whole, "root_sb", [P, KC, C])
        rw2_sb = sbuf(whole, "rw2_sb", [P, EXPERTS])
        rb2_sb = sbuf(whole, "rb2_sb", [P, EXPERTS])
        b3_sb = sbuf(whole, "b3_sb", [EXPERTS, C])
        ident = sbuf(whole, "ident", [P, P])
        head_mask = sbuf(whole, "head_mask", [P, P])
        iota_w = sbuf(whole, "iota_w", [P, WIN])
        ones = sbuf(whole, "ones", [P, P])
        eps_ln = sbuf(whole, "eps_ln", [P, 1])
        eps_den = sbuf(whole, "eps_den", [P, 1])
        BQ, GB, BO, RB1, EB1, EB2, NB = 0, 2, 4, 6, 7, 19, 31
        bias_rows = sbuf(whole, "bias_rows", [32, P])
        bias_t = sbuf(whole, "bias_t", [P, 32])
        out_bias = sbuf(whole, "out_bias", [P, KC])
        dst_t = sbuf(whole, "dst_t", [P, TILES])
        coef_t = sbuf(whole, "coef_t", [P, TILES])
        idx_t = sbuf(whole, "idx_t", [P, TILES], I32)
        vmin_b = sbuf(whole, "vmin_b", [P, BLOCKS])
        lo_row = sbuf(whole, "lo_row", [1, SUPER], I32)
        hi_row = sbuf(whole, "hi_row", [1, SUPER], I32)
        nwin_row = sbuf(whole, "nwin_row", [1, BLOCKS], I32)
        nwx_row = sbuf(whole, "nwx_row", [1, BLOCKS], I32)
        nwf_row = sbuf(whole, "nwf_row", [1, BLOCKS])
        nwu_row = sbuf(whole, "nwu_row", [1, STEPS], I32)
        kv_bd = sbuf(whole, "kv_bd", [P, KC, P])
        ksum_bd = sbuf(whole, "ksum_bd", [P, KC, P])

        pro = ExitStack()
        early = ExitStack()
        rel0_t = sbuf(early, "rel0_t", [P, TILES])
        base0_row = sbuf(early, "base0_row", [1, BLOCKS], I32)
        wrel_sb = sbuf(early, "wrel_sb", [P, KC, REL, C])
        iota_r = sbuf(early, "iota_r", [P, DR])
        iota_p = sbuf(early, "iota_p", [DR, 1])
        byte_mask = sbuf(early, "byte_mask", [DR, 1], I32)
        digits = sbuf(early, "digits", [DR, N + WIN], BF16)
        till_a = ExitStack()
        type_t = sbuf(till_a, "type_t", [P, TILES], BF16)
        with pro:
            BC = 4
            LAST = BLOCKS - 3 * P
            FULL = E // BE - 3 * P
            REST = E - (E // BE) * BE
            raw_i = sbuf(pro, "raw_i", [P, 3, BC, BE], I32)
            f_rows = sbuf(pro, "f_rows", [P, 3, BC, BE])
            w_rows = sbuf(pro, "w_rows", [P, BC, BE])
            neg_i = sbuf(pro, "neg_i", [P, P], I32)
            vmm = sbuf(pro, "vmm", [P, 2, BC])
            diag = sbuf(pro, "diag", [P, 2, BC, P])
            vmax_b = sbuf(pro, "vmax_b", [P, BLOCKS])
            digit_is = sbuf(pro, "digit_is", [DR, DIGITS])
            mask_f = sbuf(pro, "mask_f", [DR, 1])
            sstart = sbuf(pro, "sstart", [P, 1])
            send = sbuf(pro, "send", [P, 1])
            bid = sbuf(pro, "bid", [P, BLOCKS])
            below = sbuf(pro, "below", [P, BLOCKS])
            over = sbuf(pro, "over", [P, BLOCKS])
            cand = sbuf(pro, "cand", [P, 2, BLOCKS])
            lohi = sbuf(pro, "lohi", [P, 2])
            some = sbuf(pro, "some", [P, 1])
            span = sbuf(pro, "span", [1, BLOCKS])
            span_i = sbuf(pro, "span_i", [1, BLOCKS], I32)
            nw_f = sbuf(pro, "nw_f", [1, BLOCKS])
            nwu_f = sbuf(pro, "nwu_f", [1, STEPS])
            tp = [psum(pro, f"tp{i}") for i in range(2)]
            pmin, pmax, prow, pbias = (psum(pro, n) for n in ("pmin", "pmax", "prow", "pbias"))

            edges_in, pads_set, weights_in, small_in, ty_in = (
                sem(n) for n in ("edges_in", "pads_set", "weights_in", "small_in", "ty_in"))
            ident_set, consts_set, rows_done, vmm_done = (
                sem(n) for n in ("ident_set", "consts_set", "rows_done", "vmm_done"))
            tp_full, tp_free, spread_done, row_ready, row_done, bias_full = (
                sem(n) for n in ("tp_full", "tp_free", "spread_done", "row_ready", "row_done", "bias_full"))

            flat_n = 3 * P * BE

            def by_block(a):
                return a[0:flat_n].rearrange("(c p k) -> p c k", p=P, k=BE)

            block = pro.enter_context(nc.Block())

            @block.sync
            def _(sp):
                sp.wait_ge(pads_set, 1)
                n = 0
                for i, a in enumerate((dst, etype, src)):
                    sp.dma_start(raw_i[:, i, 0:3, :], by_block(a)).then_inc(edges_in, 16)
                    sp.dma_start(raw_i[0:FULL, i, 3, :],
                                 a[flat_n:flat_n + FULL * BE].rearrange("(p k) -> p k", k=BE)).then_inc(edges_in, 16)
                    sp.dma_start(raw_i[FULL:FULL + 1, i, 3, 0:REST],
                                 a[E - REST:E].rearrange("(p k) -> p k", p=1)).then_inc(edges_in, 16)
                    n += 3
                sp.dma_start(raw_i[FULL:FULL + 1, 0, 3, REST:BE],
                             dst[E - (BE - REST):E].rearrange("(p k) -> p k", p=1)).then_inc(edges_in, 16)
                sp.dma_start(w_rows[:, 0:3, :], by_block(ew)).then_inc(edges_in, 16)
                sp.dma_start(w_rows[0:FULL, 3, :],
                             ew[flat_n:flat_n + FULL * BE].rearrange("(p k) -> p k", k=BE)).then_inc(edges_in, 16)
                sp.dma_start(w_rows[FULL:FULL + 1, 3, 0:REST],
                             ew[E - REST:E].rearrange("(p k) -> p k", p=1)).then_inc(edges_in, 16)
                pad = BLOCKS * BE - E
                rows = 48
                sp.dma_start(ty_tab[0:E].rearrange("(a k) -> a k", a=16),
                             etype.rearrange("(a k) -> a k", a=16)).then_inc(ty_in, 16)
                sp.dma_start(ty_tab[E:BLOCKS * BE].rearrange("(a k) -> a k", a=rows),
                             neg_i[0:rows, 0:pad // rows]).then_inc(ty_in, 16)
                sp.wait_ge(ty_in, 32)

            EDGES_IN = 16 * 13

            @block.scalar
            def _(act):
                def two(w):
                    return w.rearrange("(k p) n -> p k n", p=P)
                act.dma_start(bias_rows[BQ:BQ + 2, :], bq.rearrange("(k p) -> k p", p=P)).then_inc(small_in, 16)
                act.dma_start(bias_rows[GB:GB + 2, :], g_b.rearrange("(k p) -> k p", p=P)).then_inc(small_in, 16)
                act.dma_start(bias_rows[BO:BO + 2, :], bo.rearrange("(k p) -> k p", p=P)).then_inc(small_in, 16)
                act.dma_start(bias_rows[RB1:RB1 + 1, :], r_b1.rearrange("(k p) -> k p", p=P)).then_inc(small_in, 16)
                act.dma_start(bias_rows[EB1:EB1 + 12, :], e_b1.rearrange("e (k p) -> (e k) p", p=P)).then_inc(small_in, 16)
                act.dma_start(bias_rows[EB2:EB2 + 12, :], e_b2.rearrange("e (k p) -> (e k) p", p=P)).then_inc(small_in, 16)
                act.dma_start(rb2_sb[:, :], r_b2.rearrange("(a n) -> a n", a=1).to_broadcast([P, EXPERTS])).then_inc(weights_in, 16)
                act.dma_start(wq_sb[:, :, :], two(wq)).then_inc(weights_in, 16)
                act.dma_start(wo_sb[:, :, :], two(wo)).then_inc(weights_in, 16)
                act.dma_start(root_sb[:, :, :], two(g_root)).then_inc(weights_in, 16)
                act.dma_start(rw2_sb[:, :], r_w2).then_inc(weights_in, 16)
                act.dma_start(b3_sb[:, :], e_b3).then_inc(weights_in, 16)
                for k in range(KC):
                    act.dma_start(wrel_sb[:, k, :, :],
                                  g_w[:, k * P:(k + 1) * P, :].rearrange("r p n -> p r n")).then_inc(weights_in, 16)
                for w_d, w_s in ((e_w2, w2_sb), (e_w3, w3_sb)):
                    for k in range(KC):
                        act.dma_start(w_s[:, :, k, :],
                                      w_d[:, k * P:(k + 1) * P, :].rearrange("e p n -> p e n")).then_inc(weights_in, 16)
                act.wait_ge(weights_in, 16 * (6 + 2 + 4))

            @block.gpsimd
            def _(pool):
                pool.memset(raw_i[:, :, 3, :], -1)
                pool.memset(neg_i[:, :], -1)
                pool.memset(w_rows[:, 3, :], 0.0).then_inc(pads_set, 1)
                pool.memset(ident[:, :], 0.0).then_inc(ident_set, 1)
                pool.wait_ge(ident_set, 1)
                pool.affine_select(out=ident[:, :], in_=ident[:, :], compare_op=ALU.not_equal, fill=1.0,
                                   base=0, pattern=[[-1, P]], channel_multiplier=1).then_inc(ident_set, 1)
                pool.memset(ones[:, :], 1.0)
                pool.memset(eps_ln[:, :], LN_EPS)
                pool.memset(eps_den[:, :], DEN_EPS)
                pool.memset(head_mask[:, :], 0.0)
                pool.iota(iota_w[:, :], pattern=[[1, WIN]], base=0, channel_multiplier=0,
                          allow_small_or_imprecise_dtypes=True)
                pool.iota(iota_r[:, :], pattern=[[0, DIGITS], [1, REL]], base=0, channel_multiplier=0,
                          allow_small_or_imprecise_dtypes=True)
                pool.iota(iota_p[:, :], pattern=[[0, 1]], base=0, channel_multiplier=1,
                          allow_small_or_imprecise_dtypes=True)
                pool.iota(sstart[:, :], pattern=[[0, 1]], base=0, channel_multiplier=NS,
                          allow_small_or_imprecise_dtypes=True)
                pool.iota(send[:, :], pattern=[[0, 1]], base=NS, channel_multiplier=NS,
                          allow_small_or_imprecise_dtypes=True)
                pool.iota(bid[:, :], pattern=[[1, BLOCKS]], base=0, channel_multiplier=0,
                          allow_small_or_imprecise_dtypes=True).then_inc(consts_set, 1)

            @block.vector
            def _(dve):
                dve.wait_ge(edges_in, EDGES_IN)
                dve.wait_ge(consts_set, 1)
                dve.wait_ge(ident_set, 2)
                for d in range(1, DIGITS):
                    dve.tensor_scalar(digit_is[:, d:d + 1], iota_p[:, :], float(d * REL), None, ALU.is_ge)
                dve.memset(mask_f[:, :], 255.0)
                dve.drain()
                for d in range(1, DIGITS):
                    dve.scalar_tensor_tensor(out=mask_f[:, :], in0=digit_is[:, d:d + 1],
                                             scalar=float(255 * (256 ** d - 256 ** (d - 1))),
                                             in1=mask_f[:, :], op0=ALU.mult, op1=ALU.add)
                    dve.scalar_tensor_tensor(out=iota_p[:, :], in0=digit_is[:, d:d + 1], scalar=-float(REL),
                                             in1=iota_p[:, :], op0=ALU.mult, op1=ALU.add)
                    dve.drain()
                dve.tensor_copy(byte_mask[:, :], mask_f[:, :])
                dve.tensor_copy(f_rows[:, 0, :, :], raw_i[:, 0, :, :])
                dve.tensor_copy(f_rows[:, 1, :, :], raw_i[:, 1, :, :])
                dve.drain()
                dve.scalar_tensor_tensor(out=f_rows[:, 2, :, :], in0=f_rows[:, 1, :, :], scalar=float(N),
                                         in1=raw_i[:, 2, :, :], op0=ALU.mult, op1=ALU.add)
                for h in range(4):
                    dve.memset(head_mask[32 * h:32 * h + 32, 32 * h:32 * h + 32], 1.0)
                dve.drain()
                dve.tensor_scalar(f_rows[:, 2, :, :], f_rows[:, 2, :, :], 0.0, None, ALU.max).then_inc(rows_done, 1)
                dve.tensor_reduce(vmm[:, 0, :], f_rows[:, 0, :, :], AX.X, ALU.min)
                dve.tensor_reduce(vmm[:, 1, :], f_rows[:, 0, :, :], AX.X, ALU.max)
                dve.drain()
                for i in range(2):
                    for c in range(BC):
                        last = dve.tensor_scalar(diag[:, i, c, :], ident[:, :], vmm[:, i, c:c + 1], None, ALU.mult)
                last.then_inc(vmm_done, 1)
                n = 0
                for c in range(BC):
                    nb = P if c < 3 else LAST
                    for a, dest in enumerate((dst_t, type_t, idx_t, coef_t)):
                        dve.wait_ge(tp_full, n + 1)
                        o = dest[:, c * BE:c * BE + nb * BT].rearrange("p (b q) -> p q b", q=BT)
                        i = tp[n % 2][:, :].rearrange("p (q b) -> p q b", q=BT)[:, :, 0:nb]
                        dve.tensor_copy(o, i).then_inc(tp_free, 1)
                        n += 1
                dve.wait_ge(spread_done, 1)
                dve.tensor_scalar(vmin_b[:, :], pmin[:, 0:BLOCKS], 0.0, None, ALU.max)
                dve.tensor_copy(vmax_b[:, :], pmax[:, 0:BLOCKS])
                dve.drain()
                dve.tensor_tensor(rel0_t[:, :].rearrange("p (b t) -> p b t", t=BT),
                                  dst_t[:, :].rearrange("p (b t) -> p b t", t=BT),
                                  vmin_b[:, :].unsqueeze(2).to_broadcast([P, BLOCKS, BT]), ALU.subtract)
                dve.tensor_copy(base0_row[:, :], vmin_b[0:1, :])
                dve.tensor_scalar(below[:, :], vmin_b[:, :], send[:, 0:1], None, ALU.is_lt)
                dve.drain()
                dve.scalar_tensor_tensor(out=over[:, :], in0=vmax_b[:, :], scalar=sstart[:, 0:1],
                                         in1=below[:, :], op0=ALU.is_ge, op1=ALU.mult)
                dve.drain()
                dve.scalar_tensor_tensor(out=cand[:, 0, :], in0=over[:, :], scalar=-1000.0, in1=bid[:, :],
                                         op0=ALU.mult, op1=ALU.add)
                dve.scalar_tensor_tensor(out=cand[:, 1, :], in0=bid[:, :], scalar=1.0, in1=over[:, :],
                                         op0=ALU.add, op1=ALU.mult)
                dve.drain()
                dve.tensor_reduce(lohi[:, 0:1], cand[:, 0, :], AX.X, ALU.min)
                dve.tensor_reduce(lohi[:, 1:2], cand[:, 1, :], AX.X, ALU.max)
                dve.drain()
                dve.tensor_scalar(some[:, :], lohi[:, 1:2], 1.0, None, ALU.min)
                dve.tensor_scalar(lohi[:, 0:1], lohi[:, 0:1], 1000.0, None, ALU.add)
                dve.drain()
                dve.tensor_tensor(lohi[:, 0:1], lohi[:, 0:1], some[:, :], ALU.mult)
                dve.drain()
                dve.tensor_scalar(lohi[:, 0:1], lohi[:, 0:1], float(BLOCKS - RANGE), None, ALU.min)
                dve.drain()
                dve.scalar_tensor_tensor(out=lohi[:, 1:2], in0=lohi[:, 0:1], scalar=float(RANGE), in1=lohi[:, 1:2],
                                         op0=ALU.add, op1=ALU.max).then_inc(row_ready, 1)
                dve.tensor_tensor(span[:, :], vmax_b[0:1, :], vmin_b[0:1, :], ALU.subtract)
                dve.drain()
                dve.tensor_scalar(span_i[:, :], span[:, :], 0.0, None, ALU.max)
                dve.drain()
                dve.tensor_single_scalar(span_i[:, :], span_i[:, :], WIN.bit_length() - 1, op=ALU.arith_shift_right)
                dve.drain()
                dve.tensor_scalar(nw_f[:, :], span_i[:, :], 1.0, None, ALU.add)
                dve.drain()
                dve.tensor_scalar(nwin_row[:, :], nw_f[:, :], float(MAXW), None, ALU.min)
                dve.tensor_scalar(nwf_row[:, :], nw_f[:, :], float(MAXW), None, ALU.min)
                dve.tensor_scalar(nwx_row[:, :], nw_f[:, :], 2.0, float(MAXW), ALU.max, ALU.min)
                dve.tensor_reduce(nwu_f[:, :], nw_f[:, :].rearrange("p (u b) -> p u b", b=UNIT), AX.X, ALU.max)
                dve.drain()
                dve.tensor_copy(nwu_row[:, :], nwu_f[:, :])
                dve.wait_ge(row_done, 1)
                dve.tensor_copy(lo_row[:, :], prow[0:1, 0:SUPER])
                dve.tensor_copy(hi_row[:, :], prow[0:1, 32:32 + SUPER])
                dve.wait_ge(bias_full, 1)
                dve.tensor_copy(bias_t[:, 0:NB], pbias[:, 0:NB])
                dve.drain()
                dve.tensor_tensor(out_bias[:, :], bias_t[:, GB:GB + 2], bias_t[:, BO:BO + 2], ALU.add)

            @block.tensor
            def _(pe):
                pe.wait_ge(ident_set, 2)
                pe.wait_ge(consts_set, 1)
                pe.wait_ge(small_in, 16 * 6)
                pe.transpose(pbias[:, 0:NB], bias_rows[0:NB, :], ident[0:NB, 0:NB]).then_inc(bias_full, 1)
                pe.wait_ge(rows_done, 1)
                n = 0
                for c in range(BC):
                    nb = P if c < 3 else LAST
                    for a in range(4):
                        if n >= 2:
                            pe.wait_ge(tp_free, n - 1)
                        for q in range(BT):
                            s_ = (f_rows[0:nb, a, c, q * P:(q + 1) * P] if a < 3
                                  else w_rows[0:nb, c, q * P:(q + 1) * P])
                            last = pe.transpose(tp[n % 2][:, q * P:q * P + nb], s_, ident[0:nb, 0:nb])
                        last.then_inc(tp_full, 1)
                        n += 1
                pe.wait_ge(vmm_done, 1)
                for i, bank in enumerate((pmin, pmax)):
                    for c in range(BC):
                        nb = P if c < 3 else LAST
                        last = pe.matmul(bank[:, c * P:c * P + nb], ones[0:nb, :], diag[0:nb, i, c, 0:nb],
                                         start=True, stop=True)
                last.then_inc(spread_done, 1)
                pe.wait_ge(row_ready, 1)
                for i in range(2):
                    last = pe.matmul(prow[0:1, 32 * i:32 * i + SUPER], lohi[0:SUPER, i:i + 1],
                                     ident[0:SUPER, 0:SUPER], start=True, stop=True)
                last.then_inc(row_done, 1)

        pa = ExitStack()
        with pa:
            cnt = sbuf(pa, "cnt", [DR, N + WIN], I32)
            wkv_sb = sbuf(pa, "wkv_sb", [P, KC, 2 * C])
            bkv_sb = sbuf(pa, "bkv_sb", [P, 2 * C])
            xs = sbuf(pa, "xs", [P, SUB, C])
            stats = sbuf(pa, "stats", [P, SUB, 6])
            mv = sbuf(pa, "mv", [P, SUB, 2])
            std = sbuf(pa, "std", [P, SUB])
            rstd = sbuf(pa, "rstd", [P, SUB])
            nmr = sbuf(pa, "nmr", [P, SUB])
            xn = sbuf(pa, "xn", [P, SUB, C])
            xnt = sbuf(pa, "xnt", [P, KC, NP])
            zk = sbuf(pa, "zk", [P, 2, C])
            vx = sbuf(pa, "vx", [P, 2, KC, P + 1])
            ek = sbuf(pa, "ek", [P, 2, C])
            rk = sbuf(pa, "rk", [P, 2, C])
            kf = sbuf(pa, "kf", [P, 2, C])
            wofs = sbuf(pa, "wofs", [P, 1])
            basew = sbuf(pa, "basew", [P, UNIT])
            base_i = sbuf(pa, "base_i", [1, UNIT], I32)
            rel = sbuf(pa, "rel", [P, UT])
            sel = sbuf(pa, "sel", [P, UT, WIN], BF16)
            rsel = sbuf(pa, "rsel", [P, UT, DR], BF16)
            zero = sbuf(pa, "zero", [P, 2 * (P + 1)])
            tb = [psum(pa, f"tb{k}") for k in range(KC)]
            pproj = [psum(pa, f"pproj{i}") for i in range(2)]
            pkv, pcnt = (psum(pa, n) for n in ("pkv", "pcnt"))

            x_in, var_ready, std_ready, nmr_ready, xn_ready, tr_done, xnt_ready, xnt_stored = (
                sem(n) for n in ("x_in", "var_ready", "std_ready", "nmr_ready", "xn_ready", "tr_done", "xnt_ready",
                                 "xnt_stored"))
            proj_done, z_done, e_done, kf_done, kv_acc = (
                sem(n) for n in ("proj_done", "z_done", "e_done", "kf_done", "kv_acc"))
            sel_ready, cnt_mm, kv_zero, wkv_in, bkv_in = (
                sem(n) for n in ("sel_ready", "cnt_mm", "kv_zero", "wkv_in", "bkv_in"))

            masked = sem("masked")
            COUNT_PARTS = 4
            CP = (N + WIN) // COUNT_PARTS

            block = pa.enter_context(nc.Block())

            @block.sync
            def _(sp):
                def load(s):
                    sp.dma_start(xs[0:NT, :, :], x[bass.ds(s * NS, NS), :].rearrange("(t p) c -> p t c", p=NT)
                                 ).then_inc(x_in, 16)

                def store(s):
                    sp.wait_ge(xnt_ready, s + 1)
                    sp.dma_start(xt_tab[bass.ds(s, 1), :, :].rearrange("a p n -> (a p) n"),
                                 xnt[:, :, :].rearrange("p k n -> p (k n)")).then_inc(xnt_stored, 16)

                sp.sem_inc(xnt_stored, 16)
                load(0)
                for i, (w, b) in enumerate(((wk, bk), (wv, bv))):
                    sp.dma_start(wkv_sb[:, :, i * C:(i + 1) * C], w.rearrange("(k p) n -> p k n", p=P)
                                 ).then_inc(wkv_in, 16)
                    sp.dma_start(bkv_sb[:, i * C:(i + 1) * C],
                                 b.rearrange("(a n) -> a n", a=1).to_broadcast([P, C])).then_inc(bkv_in, 16)
                with sp.Fori(0, SUPER - 1) as s:
                    sp.wait_ge(xn_ready, s + 1)
                    load(s + 1)
                    store(s)
                store(SUPER - 1)
                sp.wait_ge(xnt_stored, 16 * (SUPER + 1))

            @block.scalar
            def _(act):
                act.sem_inc(e_done, 2)

                def normalise(s):
                    act.wait_ge(var_ready, s + 1)
                    act.activation(std[0:NT, :], mv[0:NT, :, 1], ACT.Sqrt, bias=eps_ln[0:NT, :]).then_inc(std_ready, 1)
                    act.wait_ge(nmr_ready, s + 1)
                    for t in range(SUB):
                        last = act.activation(xn[0:NT, t, :], xs[0:NT, t, :], ACT.Identity,
                                              bias=nmr[0:NT, t:t + 1], scale=rstd[0:NT, t:t + 1])
                    last.then_inc(xn_ready, 1)

                def supertile(s, more):
                    act.wait_ge(tr_done, s + 1)
                    act.wait_ge(xnt_stored, 16 * (s + 1))
                    for k in range(KC):
                        last = act.activation(xnt[:, k, 0:NS], tb[k][:, 0:NS], ACT.Copy)
                    last.then_inc(xnt_ready, 1)
                    for t in range(SUB):
                        u = SUB * s + t
                        act.wait_ge(kf_done, u + 1)
                        act.wait_ge(z_done, u + 3)
                        act.activation(ek[0:NT, t % 2, :], zk[0:NT, t % 2, :], ACT.Exp)
                        act.activation(rk[0:NT, t % 2, :], zk[0:NT, t % 2, :], ACT.Relu).then_inc(e_done, 1)
                        if more and t == 1:
                            normalise(s + 1)

                normalise(0)
                with act.Fori(0, SUPER - 1) as s:
                    supertile(s, True)
                supertile(SUPER - 1, False)
                for c in range(COUNT_PARTS):
                    act.wait_ge(masked, c + 1)
                    act.activation(digits[:, c * CP:(c + 1) * CP], cnt[:, c * CP:(c + 1) * CP], ACT.Copy)

            @block.gpsimd
            def _(pool):
                pool.sem_inc(kf_done, 2)
                steps = pool.alloc_register("kf_steps")
                pool.reg_mov(steps, 1)
                with pool.Fori(0, SUPER) as s:
                    for t in range(SUB):
                        h = t % 2
                        n = pool.snap(steps, min_val=1, max_val=STEPS)
                        pool.wait_ge(kv_acc, n)
                        pool.wait_ge(e_done, n + 2)
                        pool.reg_add(steps, steps, 1)
                        pool.tensor_scalar(ek[0:NT, h, :], ek[0:NT, h, :], 1.0, 0.0, ALU.min, ALU.max)
                        pool.drain()
                        pool.tensor_tensor(kf[0:NT, h, :], ek[0:NT, h, :], rk[0:NT, h, :], ALU.add).then_inc(kf_done, 1)

            @block.vector
            def _(dve):
                dve.memset(cnt[:, :], 0)
                dve.memset(xnt[:, :, NS:NP], 0.0)
                dve.memset(vx[:, :, :, :], 1.0)
                dve.memset(zero[:, :], 0.0).then_inc(kv_zero, 1)
                dve.sem_inc(z_done, 2)
                qa = dve.alloc_register("count_passes")
                dve.reg_mov(qa, 1)

                def statistics(s):
                    dve.wait_ge(x_in, 16 * (s + 1))
                    for t in range(SUB):
                        dve.bn_stats(stats[0:NT, t, :], xs[0:NT, t, :])
                    dve.drain()
                    for t in range(SUB):
                        last = dve.bn_aggr(mv[0:NT, t, :], stats[0:NT, t, :])
                    last.then_inc(var_ready, 1)

                def scales(s):
                    dve.wait_ge(std_ready, s + 1)
                    dve.reciprocal(rstd[0:NT, :], std[0:NT, :])
                    dve.drain()
                    dve.scalar_tensor_tensor(out=nmr[0:NT, :], in0=mv[0:NT, :, 0], scalar=-1.0, in1=rstd[0:NT, :],
                                             op0=ALU.mult, op1=ALU.mult).then_inc(nmr_ready, 1)

                def select(u, rel_ap):
                    dve.tensor_tensor(sel[:, :, :], iota_w[:, :].unsqueeze(1).to_broadcast([P, UT, WIN]),
                                      rel_ap.unsqueeze(2).to_broadcast([P, UT, WIN]), ALU.is_equal)
                    dve.tensor_tensor(rsel[:, :, :], iota_r[:, :].unsqueeze(1).to_broadcast([P, UT, DR]),
                                      type_t[:, bass.ds(UT * u, UT)].unsqueeze(2).to_broadcast([P, UT, DR]),
                                      ALU.is_equal).then_inc(sel_ready, 1)

                def add_counts(starts):
                    q = dve.snap(qa, min_val=1, max_val=1 << 24)
                    dve.wait_ge(cnt_mm, q)
                    dve.reg_add(qa, qa, 1)
                    for b in range(UNIT):
                        here = cnt[:, bass.ds(starts[b], WIN)]
                        dve.tensor_tensor(here, here, pcnt[0:DR, b * WIN:(b + 1) * WIN], ALU.add)
                        dve.drain()

                def supertile(s, more):
                    for t in range(SUB):
                        u = SUB * s + t
                        h = t % 2
                        select(u, rel0_t[:, bass.ds(UT * u, UT)])
                        dve.wait_ge(proj_done, u + 1)
                        dve.wait_ge(kv_acc, u + 1)
                        dve.wait_ge(e_done, u + 1)
                        dve.tensor_tensor(zk[0:NT, h, :], pproj[h][0:NT, 0:C], bkv_sb[0:NT, 0:C], ALU.add)
                        dve.tensor_tensor(vx[0:NT, h, :, 0:P],
                                          pproj[h][0:NT, C:2 * C].rearrange("p (k n) -> p k n", k=KC),
                                          bkv_sb[0:NT, C:2 * C].rearrange("p (k n) -> p k n", k=KC),
                                          ALU.add).then_inc(z_done, 1)
                        if more and t == 0:
                            statistics(s + 1)
                        if more and t == 1:
                            scales(s + 1)
                        starts = load_row(dve, base0_row[0:1, bass.ds(UNIT * u, UNIT)], 0, N)
                        nw = dve.value_load(nwu_row[0:1, bass.ds(u, 1)], min_val=1, max_val=N)
                        add_counts(starts)
                        with dve.If(nw > 1):
                            dve.memset(wofs[:, :], float(WIN))
                            dve.drain()
                            with dve.Fori(1, nw):
                                dve.tensor_scalar(basew[:, :], vmin_b[:, bass.ds(UNIT * u, UNIT)], wofs[:, 0:1],
                                                  float(N), ALU.add, ALU.min)
                                dve.drain()
                                dve.tensor_scalar(wofs[:, :], wofs[:, :], float(WIN), None, ALU.add)
                                dve.tensor_copy(base_i[:, :], basew[0:1, :])
                                dve.tensor_tensor(rel[:, :].rearrange("p (b t) -> p b t", t=BT),
                                                  dst_t[:, bass.ds(UT * u, UT)].rearrange("p (b t) -> p b t", t=BT),
                                                  basew[:, :].unsqueeze(2).to_broadcast([P, UNIT, BT]), ALU.subtract)
                                dve.drain()
                                select(u, rel[:, :])
                                add_counts(load_row(dve, base_i[0:1, :], 0, N))

                statistics(0)
                scales(0)
                dve.wait_ge(bkv_in, 32)
                with dve.Fori(0, SUPER - 1) as s:
                    supertile(s, True)
                supertile(SUPER - 1, False)
                for c in range(COUNT_PARTS):
                    part = cnt[:, c * CP:(c + 1) * CP]
                    dve.tensor_tensor(part, part, byte_mask[:, :].to_broadcast([DR, CP]), ALU.bitwise_and
                                      ).then_inc(masked, 1)
                dve.wait_ge(kv_acc, STEPS + 2)
                for k in range(KC):
                    dve.tensor_tensor(kv_bd[:, k, :], pkv[:, k * (P + 1):k * (P + 1) + P], head_mask[:, :], ALU.mult)
                    dve.tensor_scalar(ksum_bd[:, k, :], head_mask[:, :], pkv[:, k * (P + 1) + P:(k + 1) * (P + 1)],
                                      None, ALU.mult)

            @block.tensor
            def _(pe):
                pe.sem_inc(kv_acc, 2)
                pe.wait_ge(kv_zero, 1)
                pe.matmul(pkv[:, 0:2 * (P + 1)], zero[:, 0:P], zero[:, :], start=True, stop=True)
                qa = pe.alloc_register("count_passes_pe")
                pe.reg_mov(qa, 1)

                def turn(s):
                    pe.wait_ge(xn_ready, s + 1)
                    for k in range(KC):
                        for t in range(SUB):
                            last = pe.transpose(tb[k][:, t * NT:(t + 1) * NT], xn[0:NT, t, k * P:(k + 1) * P],
                                                ident[0:NT, 0:NT])
                    last.then_inc(tr_done, 1)

                def count():
                    q = pe.snap(qa, min_val=1, max_val=1 << 24)
                    pe.wait_ge(sel_ready, q)
                    pe.reg_add(qa, qa, 1)
                    for e in range(UT):
                        last = pe.matmul(pcnt[0:DR, (e // BT) * WIN:(e // BT + 1) * WIN], rsel[:, e, :],
                                         sel[:, e, :], start=(e % BT == 0), stop=(e % BT == BT - 1))
                    last.then_inc(cnt_mm, 1)

                def kv_sum(u, h):
                    pe.wait_ge(kf_done, u + 3)
                    for k in range(KC):
                        last = pe.matmul(pkv[:, k * (P + 1):(k + 1) * (P + 1)], kf[0:NT, h, k * P:(k + 1) * P],
                                         vx[0:NT, h, k, :], start=False, stop=True, skip_group_check=True)
                    last.then_inc(kv_acc, 1)

                def supertile(s, more, first):
                    for t in range(SUB):
                        u = SUB * s + t
                        if t == 0:
                            pe.wait_ge(xnt_ready, s + 1)
                        pe.wait_ge(z_done, u + 1)
                        for k in range(KC):
                            last = pe.matmul(pproj[t % 2][0:NT, :], xnt[:, k, t * NT:(t + 1) * NT], wkv_sb[:, k, :],
                                             start=(k == 0), stop=(k == KC - 1))
                        last.then_inc(proj_done, 1)
                        if more and t == SUB - 1:
                            turn(s + 1)
                        nw = pe.value_load(nwu_row[0:1, bass.ds(u, 1)], min_val=1, max_val=N)
                        count()
                        with pe.If(nw > 1):
                            with pe.Fori(1, nw):
                                count()
                        if not (first and t == 0):
                            kv_sum(u - 1, (t - 1) % 2)

                turn(0)
                pe.wait_ge(wkv_in, 32)
                supertile(0, True, True)
                with pe.Fori(1, SUPER - 1) as s:
                    supertile(s, True, False)
                supertile(SUPER - 1, False, False)
                kv_sum(STEPS - 1, (STEPS - 1) % 2)

        till_a.close()
        pb = ExitStack()
        with pb:
            xb = sbuf(pb, "xb", [P, SUB, KC, P])
            x_hi = sbuf(pb, "x_hi", [P, 2, KC, P], F32R)
            x_lo = sbuf(pb, "x_lo", [P, 2, KC, P], F32R)
            w_hi = sbuf(pb, "w_hi", [P, KC, REL, C], F32R)
            w_lo = sbuf(pb, "w_lo", [P, KC, REL, C], F32R)
            yst = sbuf(pb, "yst", [P, 2, REL, C])
            ty = sbuf(pb, "ty", [DR, 2, UT * P], I32)
            rt = sbuf(pb, "rt", [DR, 2, UT * P], BF16)
            wofs = sbuf(pb, "wofs_b", [P, 1])
            basew = sbuf(pb, "basew_b", [P, UNIT])
            base_i = sbuf(pb, "base_b", [1, UNIT], I32)
            rel = sbuf(pb, "rel_b", [P, UT])
            sel = sbuf(pb, "sel_b", [P, UT, WIN])
            got = sbuf(pb, "got_b", [P, UT])
            cnt_e = sbuf(pb, "cnt_e", [P, UT])
            inv_e = sbuf(pb, "inv_e", [P, UT])
            yb = [psum(pb, f"yb{i}") for i in range(2)]
            gb = [psum(pb, f"gb{i}") for i in range(2)]

            xb_in = [sem(f"xb_in{t}") for t in range(SUB)]
            y_mm, y_ev, rt_ready, base_ready, look_free, look_mm, unit_done = (
                sem(n) for n in ("y_mm", "y_ev", "rt_ready", "base_ready", "look_free", "look_mm", "unit_done"))
            y_out = [sem(f"y_out{i}") for i in range(2)]
            ty_row = [sem(f"ty_row{i}") for i in range(2)]
            w_hi_set, w_split, x_hi_set, x_split = (sem(n) for n in ("w_hi_set", "w_split", "x_hi_set", "x_split"))

            block = pb.enter_context(nc.Block())
            RB = REL // 2

            @block.sync
            def _(sp):
                sp.sem_inc(x_split, SUB)
                sp.sem_inc(rt_ready, 2)
                with sp.Fori(0, SUPER) as s:
                    for t in range(SUB):
                        u = SUB * s + t
                        sp.wait_ge(rt_ready, u + 1)
                        sp.dma_start(ty[:, t % 2, :], ty_tab[bass.ds(u * UT * P, UT * P)]
                                     .rearrange("(a n) -> a n", a=1).to_broadcast([DR, UT * P])
                                     ).then_inc(ty_row[t % 2], 16)
                        sp.wait_ge(x_split, SUB * s + t + 1)
                        sp.dma_start(xb[:, t, :, :],
                                     xt_tab[bass.ds(s, 1), :, :].rearrange("a p (k n) -> (a p) k n", k=KC)
                                     [:, :, t * NT:t * NT + P]).then_inc(xb_in[t], 16)

            @block.scalar
            def _(act):
                for i in range(2):
                    act.sem_inc(y_out[i], 16)
                act.sem_inc(y_ev, 2)
                act.sem_inc(y_mm, 2 * RB)

                def high(s, t):
                    act.wait_ge(xb_in[t], 16 * (s + 1))
                    act.wait_ge(y_mm, RB * (SUB * s + t + 1))
                    act.activation(x_hi[:, t % 2, :, :], xb[:, t, :, :], ACT.Copy).then_inc(x_hi_set, 1)

                for r in range(RB):
                    act.activation(w_hi[:, :, 2 * r:2 * r + 2, :], wrel_sb[:, :, 2 * r:2 * r + 2, :], ACT.Copy
                                   ).then_inc(w_hi_set, 1)

                def supertile(s, more):
                    for t in range(SUB):
                        u = SUB * s + t
                        if t < SUB - 1:
                            high(s, t + 1)
                        elif more:
                            high(s + 1, 0)
                        act.wait_ge(y_out[t % 2], 16 * (2 * s + t // 2 + 1))
                        for r in range(RB):
                            act.wait_ge(y_mm, RB * (u + 2) + r + 1)
                            act.activation(yst[0:NT, t % 2, 2 * r:2 * r + 2, :],
                                           yb[r % 2][0:NT, :].rearrange("p (r n) -> p r n", r=2),
                                           ACT.Copy).then_inc(y_ev, 1)
                        act.wait_ge(y_ev, RB * (u + 1) + 2)
                        act.dma_start(y_tab.rearrange("(r n) c -> n r c", r=REL)[bass.ds(u * NT, NT), :, :],
                                      yst[0:NT, t % 2, :, :]).then_inc(y_out[t % 2], 16)

                high(0, 0)
                with act.Fori(0, SUPER - 1) as s:
                    supertile(s, True)
                supertile(SUPER - 1, False)
                for i in range(2):
                    act.wait_ge(y_out[i], 16 * (STEPS // 2 + 1))

            @block.gpsimd
            def _(pool):
                units = pool.alloc_register("type_units")
                pool.reg_mov(units, 1)
                with pool.Fori(0, SUPER) as s:
                    for t in range(SUB):
                        n = pool.snap(units, min_val=1, max_val=STEPS)
                        pool.wait_ge(ty_row[t % 2], 16 * (2 * s + t // 2 + 1))
                        pool.wait_ge(unit_done, n)
                        pool.reg_add(units, units, 1)
                        pool.tensor_scalar(rt[:, t % 2, :], ty[:, t % 2, :], iota_p[:, 0:1], None, ALU.is_equal
                                           ).then_inc(rt_ready, 1)

            @block.vector
            def _(dve):
                dve.sem_inc(unit_done, 2)
                dve.sem_inc(look_free, 1)
                qb = dve.alloc_register("look_passes")
                dve.reg_mov(qb, 1)

                def select(rel_ap):
                    dve.tensor_tensor(sel[:, :, :], iota_w[:, :].unsqueeze(1).to_broadcast([P, UT, WIN]),
                                      rel_ap.unsqueeze(2).to_broadcast([P, UT, WIN]), ALU.is_equal)
                    dve.drain()

                def look(into):
                    q = dve.snap(qb, min_val=1, max_val=1 << 24)
                    dve.wait_ge(look_mm, q)
                    dve.reg_add(qb, qb, 1)
                    H = UT // 2
                    for i in range(2):
                        last = dve.tensor_tensor(sel[:, i * H:(i + 1) * H, :], sel[:, i * H:(i + 1) * H, :],
                                                 gb[i][:, :].rearrange("p (e w) -> p e w", w=WIN), ALU.mult)
                    last.then_inc(look_free, 1)
                    dve.drain()
                    dve.tensor_reduce(into[:, :], sel[:, :, :], AX.X, ALU.add)
                    dve.drain()

                for r in range(RB):
                    dve.wait_ge(w_hi_set, r + 1)
                    two = (slice(None), slice(None), slice(2 * r, 2 * r + 2), slice(None))
                    dve.tensor_tensor(w_lo[two], wrel_sb[two], w_hi[two].bitcast(F32), ALU.subtract).then_inc(w_split, 1)

                def low(s, t):
                    dve.wait_ge(x_hi_set, SUB * s + t + 1)
                    dve.tensor_tensor(x_lo[:, t % 2, :, :], xb[:, t, :, :], x_hi[:, t % 2, :, :].bitcast(F32),
                                      ALU.subtract).then_inc(x_split, 1)

                def supertile(s, more):
                    for t in range(SUB):
                        u = SUB * s + t
                        if t < SUB - 1:
                            low(s, t + 1)
                        elif more:
                            low(s + 1, 0)
                        nw = dve.value_load(nwu_row[0:1, bass.ds(u, 1)], min_val=1, max_val=N)
                        select(rel0_t[:, bass.ds(UT * u, UT)])
                        look(cnt_e)
                        with dve.If(nw > 1):
                            dve.memset(wofs[:, :], float(WIN))
                            dve.drain()
                            with dve.Fori(1, nw):
                                dve.tensor_scalar(basew[:, :], vmin_b[:, bass.ds(UNIT * u, UNIT)], wofs[:, 0:1],
                                                  float(N), ALU.add, ALU.min)
                                dve.drain()
                                dve.tensor_scalar(wofs[:, :], wofs[:, :], float(WIN), None, ALU.add)
                                dve.tensor_copy(base_i[:, :], basew[0:1, :]).then_inc(base_ready, 1)
                                dve.tensor_tensor(rel[:, :].rearrange("p (b t) -> p b t", t=BT),
                                                  dst_t[:, bass.ds(UT * u, UT)].rearrange("p (b t) -> p b t", t=BT),
                                                  basew[:, :].unsqueeze(2).to_broadcast([P, UNIT, BT]), ALU.subtract)
                                dve.drain()
                                select(rel[:, :])
                                look(got)
                                dve.tensor_tensor(cnt_e[:, :], cnt_e[:, :], got[:, :], ALU.add)
                                dve.drain()
                        dve.tensor_scalar(inv_e[:, :], cnt_e[:, :], 1.0, None, ALU.max)
                        dve.drain()
                        dve.reciprocal(inv_e[:, :], inv_e[:, :])
                        dve.drain()
                        dve.tensor_tensor(coef_t[:, bass.ds(UT * u, UT)], coef_t[:, bass.ds(UT * u, UT)], inv_e[:, :],
                                          ALU.mult).then_inc(unit_done, 1)

                low(0, 0)
                with dve.Fori(0, SUPER - 1) as s:
                    supertile(s, True)
                supertile(SUPER - 1, False)

            @block.tensor
            def _(pe):
                qb = pe.alloc_register("look_passes_pe")
                qx = pe.alloc_register("further_passes_pe")
                for r in (qb, qx):
                    pe.reg_mov(r, 1)

                def look(t, starts):
                    q = pe.snap(qb, min_val=1, max_val=1 << 24)
                    pe.wait_ge(look_free, q)
                    pe.reg_add(qb, qb, 1)
                    for e in range(UT):
                        last = pe.matmul(gb[e // 8][:, (e % 8) * WIN:(e % 8 + 1) * WIN],
                                         rt[:, t % 2, e * P:(e + 1) * P],
                                         digits[:, bass.ds(starts[e // BT], WIN)], start=True, stop=True)
                    last.then_inc(look_mm, 1)

                pe.wait_ge(w_split, RB)
                with pe.Fori(0, SUPER) as s:
                    for t in range(SUB):
                        u = SUB * s + t
                        h = t % 2
                        pe.wait_ge(x_split, SUB + u + 1)
                        for r in range(RB):
                            if r == RB - 1:
                                pe.wait_ge(rt_ready, u + 3)
                            pe.wait_ge(y_ev, RB * u + r + 1)
                            parts = [(a, w, k) for k in range(KC) for a, w in ((x_hi, w_hi), (x_hi, w_lo), (x_lo, w_hi))]
                            for i, (a, w, k) in enumerate(parts):
                                last = pe.matmul(yb[r % 2][:, :], a[:, h, k, :], w[:, k, 2 * r:2 * r + 2, :],
                                                 start=(i == 0), stop=(i == len(parts) - 1))
                            last.then_inc(y_mm, 1)
                        nw = pe.value_load(nwu_row[0:1, bass.ds(u, 1)], min_val=1, max_val=N)
                        look(t, load_row(pe, base0_row[0:1, bass.ds(UNIT * u, UNIT)], 0, N))
                        with pe.If(nw > 1):
                            with pe.Fori(1, nw):
                                f = pe.snap(qx, min_val=1, max_val=1 << 24)
                                pe.wait_ge(base_ready, f)
                                pe.reg_add(qx, qx, 1)
                                look(t, load_row(pe, base_i[0:1, :], 0, N))
        early.close()
        pc = ExitStack()
        with pc:
            xc = sbuf(pc, "xc", [P, KC, NP])
            xr = sbuf(pc, "xr", [P, SUB, C])
            eq = sbuf(pc, "eq", [P, KC, NS])
            rq = sbuf(pc, "rq", [P, KC, NS])
            qf = sbuf(pc, "qf", [P, KC, NS])
            den, att = eq, rq
            res_t = sbuf(pc, "res_t", [P, KC, NS])
            x1 = sbuf(pc, "x1", [P, SUB, C])
            stats = sbuf(pc, "stats_c", [P, SUB, 6])
            mv = sbuf(pc, "mv_c", [P, SUB, 2])
            std = sbuf(pc, "std_c", [P, SUB])
            rstd = sbuf(pc, "rstd_c", [P, SUB])
            xn = sbuf(pc, "xn_c", [P, SUB, C])
            ft_hi = sbuf(pc, "ft_hi", [P, KC, NS], F32R)
            ft_lo = sbuf(pc, "ft_lo", [P, KC, NS], F32R)
            w1_hi = sbuf(pc, "w1_hi", [P, EXPERTS, KC, C], F32R)
            w1_lo = sbuf(pc, "w1_lo", [P, EXPERTS, KC, C], F32R)
            rw1_hi = sbuf(pc, "rw1_hi", [P, KC, P], F32R)
            rw1_lo = sbuf(pc, "rw1_lo", [P, KC, P], F32R)
            rh = sbuf(pc, "rh", [P, NS])
            h1 = sbuf(pc, "h1", [P, 2, KC, NS])
            h2 = sbuf(pc, "h2", [P, 2, KC, NS])
            y = sbuf(pc, "y", [P, SUB, C])
            lg = sbuf(pc, "lg", [P, SUB, EXPERTS])
            lmax = sbuf(pc, "lmax", [P, SUB])
            ex = sbuf(pc, "ex", [P, SUB, EXPERTS])
            esum = sbuf(pc, "esum", [P, SUB])
            probs = sbuf(pc, "probs", [P, SUB, 8])
            top = sbuf(pc, "top", [P, SUB, 8])
            top_i = sbuf(pc, "top_i", [P, SUB, 8], mybir.dt.uint32)
            top_f = sbuf(pc, "top_f", [P, SUB, 2])
            gap = sbuf(pc, "gap", [P, SUB])
            rw = sbuf(pc, "rw", [P, 2, SUB])
            hot = sbuf(pc, "hot", [P, 2, SUB, 8])
            gate = sbuf(pc, "gate", [P, SUB, 8])
            gate_t = sbuf(pc, "gate_t", [8, NS])
            ring = sbuf(pc, "ring", [P, GROUPS, CT, C])
            ring_i = sbuf(pc, "ring_i", [P, GROUPS, CT], I32)
            sc = sbuf(pc, "sc", [P, GROUPS, CT, WIN])
            first_w = sbuf(pc, "first_w", [P, RANGE])
            rel_w = sbuf(pc, "rel_w", [P, RANGE * BT])
            coef_w = sbuf(pc, "coef_w", [P, RANGE * BT])
            far_f = sbuf(pc, "far_f", [1, 1])
            tab = sbuf(pc, "tab", [1, RANGE + 1], I32)
            s_lo = sbuf(pc, "s_lo", [P, 1])
            s_top = sbuf(pc, "s_top", [P, 1])
            xring = sbuf(pc, "xring", [P, BT, C])
            xring_i = sbuf(pc, "xring_i", [P, BT], I32)
            xsc = sbuf(pc, "xsc", [P, BT, WIN])
            wofs = sbuf(pc, "wofs_c", [P, 1])
            first_x = sbuf(pc, "first_x", [P, 1])
            thr = sbuf(pc, "thr", [P, 1])
            bw = sbuf(pc, "bw", [P, 1])
            cm = sbuf(pc, "cm", [P, BT])
            rel = sbuf(pc, "rel_c", [P, BT])
            col_x = sbuf(pc, "col_x", [1, 1], I32)
            acc = [psum(pc, f"acc{k}") for k in range(KC)]
            NBANK = 6
            bank = [psum(pc, f"bank{i}") for i in range(NBANK)]

            mix_items = [("q", m, "act") for m in range(KC)]
            for k in range(KC):
                mix_items += [("den", k, "act"), ("num", k, "dve")]
            assert len(mix_items) == NBANK
            x1_items = [("x1", i, "dve") for i in range(2)]
            ft_items = [("ft", k, "dve") for k in range(KC)]
            ffn_items = [("rh", 0, "act")]
            ffn_items += [("h1", (0, m), "act") for m in range(KC)] + [("lg", 0, "dve")]
            for e in range(1, EXPERTS + 2):
                if e < EXPERTS:
                    ffn_items += [("h1", (e, m), "act") for m in range(KC)]
                if e == 2:
                    ffn_items += [("gt", 0, "act")]
                if e - 1 < EXPERTS:
                    ffn_items += [("h2", (e - 1, m), "act") for m in range(KC)]
                if e == 2:
                    ffn_items += [("b3", i, "dve") for i in range(2)]
                if e >= 2:
                    ffn_items += [("w3", (e - 2, i), "dve") for i in range(2)]
            loop_items = x1_items + mix_items[:4] + ft_items + mix_items[4:] + ffn_items
            M = len(loop_items)
            nth = {eng: sum(e == eng for _, _, e in loop_items) for eng in ("act", "dve")}
            mixed = {eng: sum(e == eng for _, _, e in mix_items) for eng in ("act", "dve")}

            def layout(items, bank0, count0, eng0):
                plan, count = {}, dict(eng0)
                for i, (kind, arg, eng) in enumerate(items):
                    count[eng] += 1
                    plan[kind, arg] = ((bank0 + i) % NBANK, count0 + i + 1, eng, count[eng])
                return plan

            LOOP = layout(loop_items, 0, 0, {"act": 0, "dve": 0})
            LAST_ONE = layout(x1_items + ft_items + ffn_items, 0, 0, {"act": 0, "dve": 0})
            FIRST = layout(mix_items, 2, M - len(mix_items), {e: nth[e] - mixed[e] for e in nth})

            items_full = sem("items_full")
            emptied = {"act": sem("act_emptied"), "dve": sem("dve_emptied")}
            qf_ready, acc_full, res_act, res_dve = (sem(n) for n in ("qf_ready", "acc_full", "res_act", "res_dve"))
            var_c, std_c, xn_c, d_ready, ex_ready, gap_ready, g2_ready, gate_ready = (
                sem(n) for n in ("var_c", "std_c", "xn_c", "d_ready", "ex_ready", "gap_ready", "g2_ready", "gate_ready"))
            y_ready, y_stored, xc_in, xr_in = (sem(n) for n in ("y_ready", "y_stored", "xc_in", "xr_in"))
            ft_hi_set, w1_split, first_in = (sem(n) for n in ("ft_hi_set", "w1_split", "first_in"))
            half = EXPERTS // 2
            staged = [b[:, :, :, :].rearrange("p a k n -> p (a k n)")[:, 0:half * KC * C]
                      .rearrange("p (e k n) -> p e k n", e=half, k=KC) for b in (h1, h2)]
            staged.append(x1[:, :, :].rearrange("p t c -> p (t c)")[:, 0:KC * P].rearrange("p (k n) -> p k n", k=KC))
            FIRST_IN = 16 * (2 * KC + 1)
            tab_ready, idx_ready, sc_ready = (sem(n) for n in ("tab_ready", "idx_ready", "sc_ready"))
            rows_in = [sem(f"rows_in{g}") for g in range(GROUPS)]
            group_used = [sem(f"group_used{g}") for g in range(GROUPS)]
            xidx_ready, xrows_in, xring_used, xsc_ready, xsc_used = (
                sem(n) for n in ("xidx_ready", "xrows_in", "xring_used", "xsc_ready", "xsc_used"))

            def full(i, plan, kind, arg):
                return (i + 1) * M + plan[kind, arg][1]

            def done(i, plan, kind, arg):
                _, _, eng, c = plan[kind, arg]
                return emptied[eng], (i + 1) * nth[eng] + c

            def uses_before(n, p):
                return (EXPERTS // GROUPS) * n + p // GROUPS + 1

            block = pc.enter_context(nc.Block())

            def leftovers(eng, lo, hi, body):
                with eng.If(lo + RANGE < hi):
                    with eng.Fori(0, hi - lo - RANGE) as i:
                        body(eng.snap(lo + RANGE + i).with_bounds(min_val=0, max_val=BLOCKS - 1))

            @block.sync
            def _(sp):
                def load_xc(s):
                    sp.dma_start(xc[:, :, :].rearrange("p k n -> p (k n)"),
                                 xt_tab[bass.ds(s, 1), :, :].rearrange("a p n -> (a p) n")).then_inc(xc_in, 16)

                def load_xr(s):
                    sp.dma_start(xr[0:NT, :, :], x[bass.ds(s * NS, NS), :].rearrange("(t p) c -> p t c", p=NT)
                                 ).then_inc(xr_in, 16)

                def store(s):
                    sp.wait_ge(y_ready, s + 1)
                    sp.dma_start(out[bass.ds(s * NS, NS), :].rearrange("(t p) c -> p t c", p=NT),
                                 y[0:NT, :, :]).then_inc(y_stored, 16)

                sp.sem_inc(y_stored, 16)
                load_xc(0)
                load_xr(0)
                for i in range(2):
                    for k in range(KC):
                        sp.dma_start(staged[i][:, :, k, :],
                                     e_w1[i * half:(i + 1) * half, k * P:(k + 1) * P, :].rearrange("e p n -> p e n")
                                     ).then_inc(first_in, 16)
                sp.dma_start(staged[2], r_w1.rearrange("(k p) n -> p k n", p=P)).then_inc(first_in, 16)
                sp.wait_ge(items_full, full(-1, FIRST, "den", 0))
                load_xc(1)
                with sp.Fori(0, SUPER - 2) as s:
                    sp.wait_ge(*done(s, LOOP, "x1", 1))
                    load_xr(s + 1)
                    sp.wait_ge(items_full, full(s, LOOP, "den", 0))
                    load_xc(s + 2)
                    store(s)
                sp.wait_ge(*done(SUPER - 2, LOOP, "x1", 1))
                load_xr(SUPER - 1)
                store(SUPER - 2)
                store(SUPER - 1)
                sp.wait_ge(y_stored, 16 * (SUPER + 1))

            @block.gpsimd
            def _(pool):
                uses = [pool.alloc_register(f"group_uses{g}") for g in range(GROUPS)]
                copies = pool.alloc_register("idx_copies")
                xuses = pool.alloc_register("leftover_uses")
                xcopies = pool.alloc_register("leftover_idx_copies")
                for r in (*uses, copies, xuses, xcopies):
                    pool.reg_mov(r, 1)

                def count(register):
                    return pool.snap(register, min_val=1, max_val=1 << 24)

                def rows(out_ap, idx_ap, signal):
                    pool.indirect_dma_start(out=out_ap, out_offset=None, in_=y_tab[:, :],
                                            in_offset=bass.IndirectOffsetOnAxis(ap=idx_ap, axis=0)
                                            ).then_inc(signal, 16)

                def leftover(blk):
                    used = count(xuses)
                    pool.wait_ge(xring_used, used)
                    pool.reg_add(xuses, xuses, 1)
                    pool.tensor_copy(xring_i[:, :], idx_t[:, bass.ds(blk * BT, BT)]).then_inc(xidx_ready, 1)
                    copied = count(xcopies)
                    pool.wait_ge(xidx_ready, copied)
                    pool.reg_add(xcopies, xcopies, 1)
                    for q in range(BT):
                        rows(xring[:, q, :], xring_i[:, q:q + 1], xrows_in)

                with pool.Fori(0, SUPER) as n:
                    lo = pool.value_load(lo_row[0:1, bass.ds(n, 1)], min_val=0, max_val=BLOCKS - RANGE)
                    hi = pool.value_load(hi_row[0:1, bass.ds(n, 1)], min_val=RANGE, max_val=BLOCKS)
                    for p in range(EXPERTS):
                        g = p % GROUPS
                        used = count(uses[g])
                        pool.wait_ge(group_used[g], used)
                        pool.reg_add(uses[g], uses[g], 1)
                        pool.tensor_copy(ring_i[:, g, :], idx_t[:, bass.ds((lo + p * CHUNK) * BT, CT)]
                                         ).then_inc(idx_ready, 1)
                        copied = count(copies)
                        pool.wait_ge(idx_ready, copied)
                        pool.reg_add(copies, copies, 1)
                        for q in range(CT):
                            rows(ring[:, g, q, :], ring_i[:, g, q:q + 1], rows_in[g])
                    leftovers(pool, lo, hi, leftover)

            @block.scalar
            def _(act):
                act.sem_inc(emptied["act"], nth["act"] - mixed["act"])

                def take(i, plan, kind, arg):
                    act.wait_ge(items_full, full(i, plan, kind, arg))
                    return bank[plan[kind, arg][0]]

                def gone(last):
                    last.then_inc(emptied["act"], 1)

                def mix(i, plan):
                    for m in range(KC):
                        b = take(i, plan, "q", m)
                        act.activation(eq[:, m, :], b[:, 0:NS], ACT.Exp, bias=bias_t[:, BQ + m:BQ + m + 1])
                        gone(act.activation(rq[:, m, :], b[:, 0:NS], ACT.Relu, bias=bias_t[:, BQ + m:BQ + m + 1]))
                    for k in range(KC):
                        b = take(i, plan, "den", k)
                        gone(act.activation(den[:, k, :], b[:, 0:NS], ACT.Identity, bias=eps_den[:, :]))
                        if k == 0 and plan is LOOP:
                            features(i, plan)

                def features(i, plan):
                    for k in range(KC):
                        b = take(i, plan, "ft", k)
                        act.activation(ft_hi[:, k, :], b[:, 0:NS], ACT.Copy).then_inc(ft_hi_set, 1)

                def iteration(i, plan):
                    def hidden(kind, e, m):
                        b = take(i, plan, kind, (e, m))
                        dest, row = (h1, EB1) if kind == "h1" else (h2, EB2)
                        gone(act.activation(dest[:, e % 2, m, :], b[:, 0:NS], ACT.Relu,
                                            bias=bias_t[:, row + KC * e + m:row + KC * e + m + 1]))

                    act.wait_ge(acc_full, i + 1)
                    act.activation(res_t[:, 0, :], acc[0][:, 0:NS], ACT.Identity, bias=out_bias[:, 0:1]
                                   ).then_inc(res_act, 1)
                    act.wait_ge(var_c, i + 1)
                    act.activation(std[0:NT, :], mv[0:NT, :, 1], ACT.Sqrt, bias=eps_ln[0:NT, :]).then_inc(std_c, 1)
                    if plan is LOOP:
                        mix(i, plan)
                    else:
                        features(i, plan)
                    b = take(i, plan, "rh", 0)
                    gone(act.activation(rh[:, :], b[:, 0:NS], ACT.Relu, bias=bias_t[:, RB1:RB1 + 1]))
                    for m in range(KC):
                        hidden("h1", 0, m)
                    for e in range(1, EXPERTS + 1):
                        if e < EXPERTS:
                            for m in range(KC):
                                hidden("h1", e, m)
                                if e == 1 and m == 0:
                                    act.wait_ge(d_ready, i + 1)
                                    act.activation(ex[0:NT, :, :], lg[0:NT, :, :], ACT.Exp).then_inc(ex_ready, 1)
                        if e == 2:
                            gone(act.activation(gate_t[:, :], take(i, plan, "gt", 0)[0:8, 0:NS], ACT.Copy))
                        for m in range(KC):
                            hidden("h2", e - 1, m)
                            if e == 1 and m == 0:
                                act.wait_ge(gap_ready, i + 1)
                                act.activation(rw[0:NT, 1, :], gap[0:NT, :], ACT.Exp).then_inc(g2_ready, 1)

                mix(-1, FIRST)
                with act.Fori(0, SUPER - 1) as s:
                    iteration(s, LOOP)
                iteration(SUPER - 1, LAST_ONE)

            @block.vector
            def _(dve):
                dve.sem_inc(emptied["dve"], nth["dve"] - mixed["dve"])
                dve.sem_inc(xsc_used, 1)
                xpasses = dve.alloc_register("further_passes_dve")
                dve.reg_mov(xpasses, 1)
                dve.memset(probs[:, :, :], -1.0)
                dve.memset(s_lo[:, :], 0.0)
                dve.memset(s_top[:, :], float(NS - WIN))
                dve.drain()

                def take(i, plan, kind, arg):
                    dve.wait_ge(items_full, full(i, plan, kind, arg))
                    return bank[plan[kind, arg][0]]

                def gone(last):
                    last.then_inc(emptied["dve"], 1)

                def attention(i, plan):
                    for k in range(KC):
                        dve.wait_ge(*done(i, plan, "q", k))
                        dve.scalar_tensor_tensor(out=qf[:, k, :], in0=eq[:, k, :], scalar=1.0, in1=rq[:, k, :],
                                                 op0=ALU.min, op1=ALU.add).then_inc(qf_ready, 1)
                    for k in range(KC):
                        dve.wait_ge(*done(i, plan, "den", k))
                        dve.reciprocal(den[:, k, :], den[:, k, :])
                        dve.drain()
                        b = take(i, plan, "num", k)
                        gone(dve.tensor_tensor(att[:, k, :], b[:, 0:NS], den[:, k, :], ALU.mult))
                        if k == 0 and plan is LOOP:
                            features(i, plan)

                def features(i, plan):
                    for k in range(KC):
                        b = bank[plan["ft", k][0]]
                        dve.wait_ge(ft_hi_set, KC * i + k + 1)
                        gone(dve.tensor_tensor(ft_lo[:, k, :], b[:, 0:NS], ft_hi[:, k, :].bitcast(F32), ALU.subtract))

                def by_tile(a, n):
                    return a.unsqueeze(2).to_broadcast([P, n, BT])

                def tables(n):
                    lo = dve.value_load(lo_row[0:1, bass.ds(n, 1)], min_val=0, max_val=BLOCKS - RANGE)
                    hi = dve.value_load(hi_row[0:1, bass.ds(n, 1)], min_val=RANGE, max_val=BLOCKS)
                    dve.tensor_scalar(first_w[:, :], vmin_b[:, bass.ds(lo, RANGE)], s_lo[:, 0:1], s_top[:, 0:1],
                                      ALU.max, ALU.min)
                    dve.tensor_copy(coef_w[:, :], coef_t[:, bass.ds(lo * BT, RANGE * BT)])
                    dve.tensor_reduce(far_f[:, :], nwf_row[0:1, bass.ds(lo, RANGE)], AX.X, ALU.max)
                    dve.drain()
                    dve.tensor_tensor(rel_w[:, :].rearrange("p (b t) -> p b t", t=BT),
                                      dst_t[:, bass.ds(lo * BT, RANGE * BT)].rearrange("p (b t) -> p b t", t=BT),
                                      by_tile(first_w[:, :], RANGE), ALU.subtract)
                    dve.tensor_scalar(tab[:, 0:RANGE], first_w[0:1, :], s_lo[0:1, 0:1], None, ALU.subtract)
                    dve.tensor_copy(tab[:, RANGE:RANGE + 1], far_f[:, :]).then_inc(tab_ready, 1)
                    dve.drain()
                    return lo, hi, dve.value_load(tab[0:1, RANGE:RANGE + 1], min_val=1, max_val=MAXW)

                def next_borders():
                    dve.tensor_scalar(s_lo[:, :], s_lo[:, :], float(NS), None, ALU.add)
                    dve.tensor_scalar(s_top[:, :], s_top[:, :], float(NS), None, ALU.add)

                def build(n, p):
                    g = p % GROUPS
                    dve.wait_ge(group_used[g], uses_before(n, p))
                    dve.tensor_tensor(sc[:, g, :, :], iota_w[:, :].unsqueeze(1).to_broadcast([P, CT, WIN]),
                                      rel_w[:, p * CT:(p + 1) * CT].unsqueeze(2).to_broadcast([P, CT, WIN]),
                                      ALU.is_equal)
                    dve.drain()
                    dve.tensor_tensor(sc[:, g, :, :], sc[:, g, :, :],
                                      coef_w[:, p * CT:(p + 1) * CT].unsqueeze(2).to_broadcast([P, CT, WIN]),
                                      ALU.mult).then_inc(sc_ready, 1)

                def windows(blk, first, count):
                    dve.memset(wofs[:, :], float(WIN * first))
                    dve.tensor_scalar(first_x[:, :], vmin_b[:, bass.ds(blk, 1)], s_lo[:, 0:1], s_top[:, 0:1],
                                      ALU.max, ALU.min)
                    dve.drain()
                    with dve.Fori(first, count):
                        dve.tensor_scalar(thr[:, :], first_x[:, :], wofs[:, 0:1], None, ALU.add)
                        dve.tensor_scalar(bw[:, :], first_x[:, :], wofs[:, 0:1], s_top[:, 0:1], ALU.add, ALU.min)
                        dve.drain()
                        dve.tensor_scalar(wofs[:, :], wofs[:, :], float(WIN), None, ALU.add)
                        dve.scalar_tensor_tensor(out=cm[:, :], in0=dst_t[:, bass.ds(blk * BT, BT)],
                                                 scalar=thr[:, 0:1], in1=coef_t[:, bass.ds(blk * BT, BT)],
                                                 op0=ALU.is_ge, op1=ALU.mult)
                        dve.tensor_scalar(rel[:, :], dst_t[:, bass.ds(blk * BT, BT)], bw[:, 0:1], None, ALU.subtract)
                        dve.drain()
                        dve.wait_ge(xsc_used, dve.snap(xpasses, min_val=1, max_val=1 << 24))
                        dve.tensor_scalar(col_x[:, :], bw[0:1, :], s_lo[0:1, 0:1], None, ALU.subtract)
                        for q in range(BT):
                            last = dve.tensor_scalar(xsc[:, q, :], iota_w[:, :], rel[:, q:q + 1], cm[:, q:q + 1],
                                                     ALU.is_equal, ALU.mult)
                        last.then_inc(xsc_ready, 1)
                        dve.drain()
                        dve.reg_add(xpasses, xpasses, 1)

                def leftover(blk):
                    windows(blk, 0, dve.value_load(nwin_row[0:1, bass.ds(blk, 1)], min_val=1, max_val=MAXW))

                def further(n, p, lo, far):
                    with dve.If(far > 1):
                        for j in range(CHUNK):
                            blk = dve.snap(lo + (p * CHUNK + j), min_val=0, max_val=BLOCKS - 1)
                            windows(blk, 1, dve.value_load(nwx_row[0:1, bass.ds(blk, 1)], min_val=2, max_val=MAXW))
                    if p + GROUPS < EXPERTS:
                        build(n, p + GROUPS)

                def iteration(i, plan):
                    dve.wait_ge(acc_full, i + 1)
                    dve.tensor_scalar(res_t[:, 1, :], acc[1][:, 0:NS], out_bias[:, 1:2], None, ALU.add
                                      ).then_inc(res_dve, 1)
                    dve.wait_ge(xr_in, 16 * (i + 1))
                    for h in range(2):
                        b = take(i, plan, "x1", h)
                        gone(dve.tensor_tensor(x1[0:NT, 2 * h:2 * h + 2, :],
                                               b[0:NT, :].rearrange("p (t c) -> p t c", t=2),
                                               xr[0:NT, 2 * h:2 * h + 2, :], ALU.add))
                    dve.drain()
                    for t in range(SUB):
                        dve.bn_stats(stats[0:NT, t, :], x1[0:NT, t, :])
                    dve.drain()
                    for t in range(SUB):
                        last = dve.bn_aggr(mv[0:NT, t, :], stats[0:NT, t, :])
                    last.then_inc(var_c, 1)
                    dve.wait_ge(std_c, i + 1)
                    dve.reciprocal(rstd[0:NT, :], std[0:NT, :])
                    dve.drain()
                    for t in range(SUB):
                        last = dve.tensor_scalar(xn[0:NT, t, :], x1[0:NT, t, :], mv[0:NT, t, 0:1], rstd[0:NT, t:t + 1],
                                                 ALU.subtract, ALU.mult)
                    last.then_inc(xn_c, 1)
                    if plan is LOOP:
                        attention(i, plan)
                    else:
                        features(i, plan)

                    def by_expert(v, n):
                        return v.unsqueeze(2).to_broadcast([NT, SUB, n])
                    b = take(i, plan, "lg", 0)
                    gone(dve.tensor_tensor(lg[0:NT, :, :],
                                           b[0:NT, 0:SUB * EXPERTS].rearrange("p (t e) -> p t e", t=SUB),
                                           rb2_sb[0:NT, :].unsqueeze(1).to_broadcast([NT, SUB, EXPERTS]), ALU.add))
                    dve.drain()
                    dve.tensor_reduce(lmax[0:NT, :], lg[0:NT, :, :], AX.X, ALU.max)
                    dve.drain()
                    dve.tensor_tensor(lg[0:NT, :, :], lg[0:NT, :, :], by_expert(lmax[0:NT, :], EXPERTS),
                                      ALU.subtract).then_inc(d_ready, 1)
                    dve.wait_ge(ex_ready, i + 1)
                    dve.tensor_reduce(esum[0:NT, :], ex[0:NT, :, :], AX.X, ALU.add)
                    dve.drain()
                    dve.reciprocal(esum[0:NT, :], esum[0:NT, :])
                    dve.drain()
                    dve.tensor_tensor(probs[0:NT, :, 0:EXPERTS], ex[0:NT, :, :], by_expert(esum[0:NT, :], EXPERTS),
                                      ALU.mult)
                    dve.drain()
                    for t in range(SUB):
                        dve.max(top[0:NT, t, :], probs[0:NT, t, :])
                    dve.drain()
                    dve.tensor_tensor(gap[0:NT, :], top[0:NT, :, 1], top[0:NT, :, 0], ALU.subtract
                                      ).then_inc(gap_ready, 1)
                    for t in range(SUB):
                        dve.max_index(top_i[0:NT, t, :], top[0:NT, t, :], probs[0:NT, t, :])
                    dve.drain()
                    dve.tensor_copy(top_f[0:NT, :, :], top_i[0:NT, :, 0:2])
                    dve.wait_ge(g2_ready, i + 1)
                    dve.tensor_scalar(rw[0:NT, 0, :], rw[0:NT, 1, :], 1.0, None, ALU.add)
                    dve.drain()
                    dve.reciprocal(rw[0:NT, 0, :], rw[0:NT, 0, :])
                    dve.drain()
                    dve.tensor_tensor(rw[0:NT, 1, :], rw[0:NT, 1, :], rw[0:NT, 0, :], ALU.mult)
                    for h in range(2):
                        dve.tensor_tensor(hot[0:NT, h, :, :],
                                          iota_w[0:NT, 0:8].unsqueeze(1).to_broadcast([NT, SUB, 8]),
                                          by_expert(top_f[0:NT, :, h], 8), ALU.is_equal)
                    dve.drain()
                    for h in range(2):
                        dve.tensor_tensor(hot[0:NT, h, :, :], hot[0:NT, h, :, :], by_expert(rw[0:NT, h, :], 8), ALU.mult)
                    dve.drain()
                    dve.tensor_tensor(gate[0:NT, :, :], hot[0:NT, 0, :, :], hot[0:NT, 1, :, :], ALU.add
                                      ).then_inc(gate_ready, 1)
                    if plan is LOOP:
                        lo, hi, far = tables(i + 1)
                        for p in range(GROUPS):
                            build(i + 1, p)
                    dve.wait_ge(y_stored, 16 * (i + 1))
                    for h in range(2):
                        b = take(i, plan, "b3", h)
                        gone(dve.tensor_tensor(y[0:NT, 2 * h:2 * h + 2, :],
                                               b[0:NT, :].rearrange("p (t c) -> p t c", t=2),
                                               x1[0:NT, 2 * h:2 * h + 2, :], ALU.add))
                    for e in range(EXPERTS):
                        dve.drain()
                        for h in range(2):
                            b = take(i, plan, "w3", (e, h))
                            for t in (2 * h, 2 * h + 1):
                                last = dve.scalar_tensor_tensor(out=y[0:NT, t, :], in0=b[0:NT, (t % 2) * C:(t % 2 + 1) * C],
                                                                scalar=gate[0:NT, t, e:e + 1], in1=y[0:NT, t, :],
                                                                op0=ALU.mult, op1=ALU.add)
                            gone(last)
                        if e == EXPERTS - 1:
                            dve.drain()
                            dve.sem_inc(y_ready, 1)
                        if plan is LOOP:
                            further(i + 1, e, lo, far)
                    if plan is LOOP:
                        leftovers(dve, lo, hi, leftover)
                        next_borders()


                attention(-1, FIRST)
                lo, hi, far = tables(0)
                for p in range(GROUPS):
                    build(0, p)
                dve.wait_ge(first_in, FIRST_IN)
                for i in range(2):
                    part = slice(i * half, (i + 1) * half)
                    dve.tensor_copy(w1_hi[:, part], staged[i])
                    dve.drain()
                    dve.tensor_tensor(w1_lo[:, part], staged[i], w1_hi[:, part].bitcast(F32), ALU.subtract)
                dve.tensor_copy(rw1_hi[:, :, :], staged[2])
                dve.drain()
                last = dve.tensor_tensor(rw1_lo[:, :, :], staged[2], rw1_hi[:, :, :].bitcast(F32), ALU.subtract)
                last.then_inc(w1_split, 1)
                for p in range(EXPERTS):
                    further(0, p, lo, far)
                leftovers(dve, lo, hi, leftover)
                next_borders()
                with dve.Fori(0, SUPER - 1) as s:
                    iteration(s, LOOP)
                iteration(SUPER - 1, LAST_ONE)

            @block.tensor
            def _(pe):
                pe.sem_inc(items_full, M - len(mix_items))
                for g in range(GROUPS):
                    pe.sem_inc(group_used[g], 1)
                pe.sem_inc(xring_used, 1)
                xpasses = pe.alloc_register("further_passes_pe_c")
                xblocks = pe.alloc_register("leftover_rows_pe")
                pe.reg_mov(xpasses, 1)
                pe.reg_mov(xblocks, 16 * BT)
                tabs, chunks = (pe.alloc_register(n) for n in ("tables_read", "chunks_added"))
                pe.reg_mov(tabs, 1)
                pe.reg_mov(chunks, 1)

                def give(i, plan, kind, arg):
                    b = plan[kind, arg][0]
                    before = [key for key, v in plan.items() if v[0] == b and v[1] < plan[kind, arg][1]]
                    if before:
                        pe.wait_ge(*done(i, plan, *before[-1]))
                    elif plan is not FIRST:
                        pe.wait_ge(*done(i - 1, LOOP, *[key for key, v in LOOP.items() if v[0] == b][-1]))
                    return bank[b]

                def filled(last):
                    last.then_inc(items_full, 1)

                def mix(i, plan):
                    pe.wait_ge(xc_in, 16 * (i + 2))
                    for m in range(KC):
                        b = give(i, plan, "q", m)
                        for k in range(KC):
                            last = pe.matmul(b[:, 0:NS], wq_sb[:, k, m * P:(m + 1) * P], xc[:, k, 0:NS],
                                             start=(k == 0), stop=(k == KC - 1))
                        filled(last)
                    for m in range(KC):
                        for k in range(KC):
                            pe.matmul(acc[m][:, 0:NS], root_sb[:, k, m * P:(m + 1) * P], xc[:, k, 0:NS],
                                      start=(k == 0), stop=False, skip_group_check=True)
                    for k in range(KC):
                        b = give(i, plan, "den", k)
                        pe.wait_ge(qf_ready, KC * (i + 1) + k + 1)
                        filled(pe.matmul(b[:, 0:NS], ksum_bd[:, k, :], qf[:, k, :], start=True, stop=True))
                        b = give(i, plan, "num", k)
                        filled(pe.matmul(b[:, 0:NS], kv_bd[:, k, :], qf[:, k, :], start=True, stop=True))
                        if k == 0 and plan is LOOP:
                            turn(i, plan)

                def turn(i, plan):
                    for k in range(KC):
                        b = give(i, plan, "ft", k)
                        pe.wait_ge(xn_c, i + 1)
                        for t in range(SUB):
                            last = pe.transpose(b[:, t * NT:(t + 1) * NT], xn[0:NT, t, k * P:(k + 1) * P],
                                                ident[0:NT, 0:NT])
                        filled(last)

                def in_parts(out_ap, hi, lo, src_hi, src_lo):
                    parts = [(a(k), b(k)) for k in range(KC) for a, b in ((hi, src_hi), (hi, src_lo), (lo, src_hi))]
                    for i, (a, b) in enumerate(parts):
                        last = pe.matmul(out_ap, a, b, start=(i == 0), stop=(i == len(parts) - 1))
                    return last

                def add_edges(col, rows, coefs):
                    for q in range(BT):
                        for k in range(KC):
                            last = pe.matmul(acc[k][:, bass.ds(col, WIN)], rows[:, q, k * P:(k + 1) * P],
                                             coefs[:, q, :], start=False, stop=False, skip_group_check=True)
                    return last

                def windows(first, count, rows):
                    with pe.Fori(first, count):
                        built = pe.snap(xpasses, min_val=1, max_val=1 << 24)
                        pe.wait_ge(xsc_ready, built)
                        pe.reg_add(xpasses, xpasses, 1)
                        col = pe.value_load(col_x[0:1, :], min_val=0, max_val=NS - WIN)
                        add_edges(col, rows, xsc).then_inc(xsc_used, 1)

                def leftover(blk):
                    nw = pe.value_load(nwin_row[0:1, bass.ds(blk, 1)], min_val=1, max_val=MAXW)
                    arrived = pe.snap(xblocks, min_val=1, max_val=1 << 24)
                    pe.wait_ge(xrows_in, arrived)
                    pe.reg_add(xblocks, xblocks, 16 * BT)
                    windows(0, nw, xring)
                    pe.drain()
                    pe.sem_inc(xring_used, 1)

                def bounds(n):
                    lo = pe.value_load(lo_row[0:1, bass.ds(n, 1)], min_val=0, max_val=BLOCKS - RANGE)
                    hi = pe.value_load(hi_row[0:1, bass.ds(n, 1)], min_val=RANGE, max_val=BLOCKS)
                    made = pe.snap(tabs, min_val=1, max_val=SUPER)
                    pe.wait_ge(tab_ready, made)
                    pe.reg_add(tabs, tabs, 1)
                    return lo, hi, pe.value_load(tab[0:1, RANGE:RANGE + 1], min_val=1, max_val=MAXW)

                def aggregate(n, p, lo, far):
                    g = p % GROUPS
                    cols = load_row(pe, tab[0:1, p * CHUNK:(p + 1) * CHUNK], 0, NS - WIN)
                    uses = (EXPERTS // GROUPS) * n + p // GROUPS
                    built = pe.snap(chunks, min_val=1, max_val=SUPER * EXPERTS)
                    pe.wait_ge(rows_in[g], 16 * CT * (uses + 1))
                    pe.wait_ge(sc_ready, built)
                    pe.reg_add(chunks, chunks, 1)
                    with pe.If(far > 1):
                        for j in range(CHUNK):
                            blk = pe.snap(lo + (p * CHUNK + j), min_val=0, max_val=BLOCKS - 1)
                            nw = pe.value_load(nwx_row[0:1, bass.ds(blk, 1)], min_val=2, max_val=MAXW)
                            windows(1, nw, ring[:, g, j * BT:(j + 1) * BT, :])
                    for j in range(CHUNK):
                        last = add_edges(cols[j], ring[:, g, j * BT:(j + 1) * BT, :], sc[:, g, j * BT:(j + 1) * BT, :])
                    last.then_inc(group_used[g], 1)

                def close_sum(i, plan):
                    pe.wait_ge(*done(i, plan, "num", KC - 1))
                    for m in range(KC):
                        for k in range(KC):
                            last = pe.matmul(acc[m][:, 0:NS], wo_sb[:, k, m * P:(m + 1) * P], att[:, k, :],
                                             start=False, stop=(k == KC - 1), skip_group_check=True)
                    last.then_inc(acc_full, 1)

                features = (lambda k: ft_hi[:, k, :]), (lambda k: ft_lo[:, k, :])

                def iteration(i, plan):
                    def hidden(kind, e, m):
                        b = give(i, plan, kind, (e, m))
                        cols = slice(m * P, (m + 1) * P)
                        if kind == "h1":
                            filled(in_parts(b[:, 0:NS], lambda k: w1_hi[:, e, k, cols],
                                            lambda k: w1_lo[:, e, k, cols], *features))
                            return
                        pe.wait_ge(*done(i, plan, "h1", (e, KC - 1)))
                        for k in range(KC):
                            last = pe.matmul(b[:, 0:NS], w2_sb[:, e, k, cols], h1[:, e % 2, k, :],
                                             start=(k == 0), stop=(k == KC - 1))
                        filled(last)

                    pe.wait_ge(res_act, i + 1)
                    pe.wait_ge(res_dve, i + 1)
                    for h in range(2):
                        b = give(i, plan, "x1", h)
                        for t in (2 * h, 2 * h + 1):
                            for k in range(KC):
                                o = (t % 2) * C + k * P
                                last = pe.transpose(b[0:NT, o:o + P], res_t[:, k, t * NT:(t + 1) * NT], ident[:, :])
                        filled(last)
                    if plan is LOOP:
                        mix(i, plan)
                    else:
                        turn(i, plan)
                    b = give(i, plan, "rh", 0)
                    pe.wait_ge(*done(i, plan, "ft", KC - 1))
                    filled(in_parts(b[:, 0:NS], lambda k: rw1_hi[:, k, :], lambda k: rw1_lo[:, k, :],
                                    *features))
                    for m in range(KC):
                        hidden("h1", 0, m)
                    b = give(i, plan, "lg", 0)
                    pe.wait_ge(*done(i, plan, "rh", 0))
                    for t in range(SUB):
                        last = pe.matmul(b[0:NT, t * EXPERTS:(t + 1) * EXPERTS], rh[:, t * NT:(t + 1) * NT],
                                         rw2_sb[:, :], start=True, stop=True)
                    filled(last)
                    for e in range(1, EXPERTS + 2):
                        if e < EXPERTS:
                            for m in range(KC):
                                hidden("h1", e, m)
                        if e == 2:
                            b = give(i, plan, "gt", 0)
                            pe.wait_ge(gate_ready, i + 1)
                            for t in range(SUB):
                                last = pe.transpose(b[0:8, t * NT:(t + 1) * NT], gate[0:NT, t, :], ident[0:NT, 0:NT])
                            filled(last)
                        if e - 1 < EXPERTS:
                            for m in range(KC):
                                hidden("h2", e - 1, m)
                        if e == 2:
                            pe.wait_ge(*done(i, plan, "gt", 0))
                            for h in range(2):
                                b = give(i, plan, "b3", h)
                                for t in (2 * h, 2 * h + 1):
                                    last = pe.matmul(b[0:NT, (t % 2) * C:(t % 2 + 1) * C],
                                                     gate_t[0:EXPERTS, t * NT:(t + 1) * NT], b3_sb[:, :],
                                                     start=True, stop=True)
                                filled(last)
                            if plan is LOOP:
                                lo, hi, far = bounds(i + 1)
                        if e >= 2:
                            pe.wait_ge(*done(i, plan, "h2", (e - 2, KC - 1)))
                            for h in range(2):
                                b = give(i, plan, "w3", (e - 2, h))
                                for t in (2 * h, 2 * h + 1):
                                    for k in range(KC):
                                        last = pe.matmul(b[0:NT, (t % 2) * C:(t % 2 + 1) * C],
                                                         h2[:, e % 2, k, t * NT:(t + 1) * NT], w3_sb[:, e - 2, k, :],
                                                         start=(k == 0), stop=(k == KC - 1))
                                filled(last)
                            if plan is LOOP:
                                aggregate(i + 1, e - 2, lo, far)
                    if plan is LOOP:
                        leftovers(pe, lo, hi, leftover)
                        close_sum(i, plan)

                mix(-1, FIRST)
                lo, hi, far = bounds(0)
                for p in range(EXPERTS):
                    aggregate(0, p, lo, far)
                leftovers(pe, lo, hi, leftover)
                close_sum(-1, FIRST)
                pe.wait_ge(w1_split, 1)
                with pe.Fori(0, SUPER - 1) as s:
                    iteration(s, LOOP)
                iteration(SUPER - 1, LAST_ONE)


_INS = ["x", "src", "dst", "edge_type_8", "edge_weight", "L0_gnn_weight", "L0_gnn_root", "L0_gnn_bias",
        "L0_mix_wq", "L0_mix_bq", "L0_mix_wk", "L0_mix_bk", "L0_mix_wv", "L0_mix_bv", "L0_mix_wo", "L0_mix_bo",
        "L0_ffn_router_w1", "L0_ffn_router_b1", "L0_ffn_router_w2", "L0_ffn_router_b2",
        "L0_ffn_expert_w1", "L0_ffn_expert_b1", "L0_ffn_expert_w2", "L0_ffn_expert_b2",
        "L0_ffn_expert_w3", "L0_ffn_expert_b3"]


def kernel(**inputs):
    import numpy as _np
    import concourse.bacc as _bacc
    from concourse import mybir as _mybir
    from concourse.bass_utils import run_bass_kernel_spmd as _run

    nc = _bacc.Bacc("TRN2", target_bir_lowering=False, num_devices=1)
    arrays, args = {}, []
    for name in _INS:
        a = _np.ascontiguousarray(inputs[name])
        arrays[f"in_{name}"] = a
        args.append(nc.dram_tensor(f"in_{name}", a.shape, _mybir.dt.from_np(a.dtype), kind="ExternalInput").ap())
    args.append(nc.dram_tensor("out_0", (12500, 256), _mybir.dt.float32, kind="ExternalOutput").ap())
    gps_layer(nc, *args)
    r = _run(nc, [arrays], core_ids=[0])
    return r.results[0]["out_0"]
```
